# Optimizing a Trainium2 kernel written in Bass

```python
import numpy as np
import jax
import jax.numpy as jnp

def _softmax(x, axis=-1):
    return jax.nn.softmax(x, axis=axis)

def _gelu(x):
    return jax.nn.gelu(x, approximate=True)

def _silu(x):
    return jax.nn.silu(x)

def _sigmoid(x):
    return jax.nn.sigmoid(x)

def _layernorm(x, axis=-1, eps=1e-05):
    m = jnp.mean(x, axis=axis, keepdims=True)
    v = jnp.var(x, axis=axis, keepdims=True)
    return (x - m) / jnp.sqrt(v + eps)

def _scatter_add(tgt, idx, src, axis=0):
    return tgt.at[idx].add(src)

def _segment_sum(src, seg, n):
    return jax.ops.segment_sum(src, seg, n)
kernel_name = 'mk_gnn_preln_d1_gnn_r8_a35705'

def setup_inputs(seed: int=0):
    np.random.seed(seed)
    _w = jnp.asarray

    def _rec_inputs():
        import jax
        import jax.numpy as jnp
        _gk = jax.random.key(seed)
        x = -0.0005121 + 1.001 * jax.random.normal(jax.random.fold_in(_gk, 1), (12500, 64), jnp.float32)
        _s = jax.random.randint(jax.random.fold_in(_gk, 2), (100000,), 0, 12500, jnp.int32)
        _d = jax.random.randint(jax.random.fold_in(_gk, 3), (100000,), 0, 12500, jnp.int32)
        _loop = jnp.arange(12500, dtype=jnp.int32)
        src = jnp.concatenate([_s, _d, _loop])
        dst = jnp.concatenate([_d, _s, _loop])
        _o = jnp.argsort(dst, stable=True)
        src = src[_o]
        dst = dst[_o]
        edge_attr_32 = 0.000283511 + 1.00007 * jax.random.normal(jax.random.fold_in(_gk, 11), (212500, 32), jnp.float32)
        return (x, src, dst, edge_attr_32)
    x, src, dst, edge_attr_32 = _rec_inputs()

    def _L0_gnn_setup():
        import math
        import jax, jax.numpy as jnp
        import numpy as np
        N_NODES = 6250
        N_EDGES = 75000
        IN_CH = 64
        HEADS = 2
        C = 64
        HC = HEADS * C
        EDGE_DIM = 32

        def _layernorm(x, g, b, eps=1e-05):
            m = jnp.mean(x, axis=-1, keepdims=True)
            v = jnp.mean(jnp.square(x - m), axis=-1, keepdims=True)
            return (x - m) / jnp.sqrt(v + eps) * g + b
        key = jax.random.key(seed)
        ks = jax.random.split(key, 12)
        s = 0.05
        return {'x': jax.random.normal(ks[0], (N_NODES, IN_CH), jnp.float32), 'edge_index': jax.random.randint(ks[1], (2, N_EDGES), 0, N_NODES, dtype=jnp.int64), 'edge_attr': jax.random.normal(ks[2], (N_EDGES, EDGE_DIM), jnp.float32), 'Wq': s * jax.random.normal(ks[3], (IN_CH, HC), jnp.float32), 'bq': jnp.zeros((HC,), jnp.float32), 'Wk': s * jax.random.normal(ks[4], (IN_CH, HC), jnp.float32), 'bk': jnp.zeros((HC,), jnp.float32), 'Wv': s * jax.random.normal(ks[5], (IN_CH, HC), jnp.float32), 'bv': jnp.zeros((HC,), jnp.float32), 'We': s * jax.random.normal(ks[6], (EDGE_DIM, HC), jnp.float32), 'Wp': s * jax.random.normal(ks[7], (HC, IN_CH), jnp.float32), 'bp': jnp.zeros((IN_CH,), jnp.float32), 'ln1_g': jnp.ones((IN_CH,), jnp.float32), 'ln1_b': jnp.zeros((IN_CH,), jnp.float32), 'ln2_g': jnp.ones((IN_CH,), jnp.float32), 'ln2_b': jnp.zeros((IN_CH,), jnp.float32), 'W1': s * jax.random.normal(ks[8], (IN_CH, IN_CH), jnp.float32), 'b1': jnp.zeros((IN_CH,), jnp.float32), 'W2': s * jax.random.normal(ks[9], (IN_CH, IN_CH), jnp.float32), 'b2': jnp.zeros((IN_CH,), jnp.float32)}
    _L0_gnn_all = _L0_gnn_setup()
    _L0_gnn_in = {k: v for k, v in _L0_gnn_all.items() if k in ('Wq', 'bq', 'Wk', 'bk', 'Wv', 'bv', 'We', 'Wp', 'bp', 'ln1_g', 'ln1_b', 'ln2_g', 'ln2_b', 'W1', 'b1', 'W2', 'b2')}
    del _L0_gnn_all
    return {'x': x, 'src': src, 'dst': dst, 'edge_attr_32': edge_attr_32, 'L0_gnn_Wq': _L0_gnn_in['Wq'], 'L0_gnn_bq': _L0_gnn_in['bq'], 'L0_gnn_Wk': _L0_gnn_in['Wk'], 'L0_gnn_bk': _L0_gnn_in['bk'], 'L0_gnn_Wv': _L0_gnn_in['Wv'], 'L0_gnn_bv': _L0_gnn_in['bv'], 'L0_gnn_We': _L0_gnn_in['We'], 'L0_gnn_Wp': _L0_gnn_in['Wp'], 'L0_gnn_bp': _L0_gnn_in['bp'], 'L0_gnn_ln1_g': _L0_gnn_in['ln1_g'], 'L0_gnn_ln1_b': _L0_gnn_in['ln1_b'], 'L0_gnn_ln2_g': _L0_gnn_in['ln2_g'], 'L0_gnn_ln2_b': _L0_gnn_in['ln2_b'], 'L0_gnn_W1': _L0_gnn_in['W1'], 'L0_gnn_b1': _L0_gnn_in['b1'], 'L0_gnn_W2': _L0_gnn_in['W2'], 'L0_gnn_b2': _L0_gnn_in['b2']}

def reference(x, src, dst, edge_attr_32, L0_gnn_Wq, L0_gnn_bq, L0_gnn_Wk, L0_gnn_bk, L0_gnn_Wv, L0_gnn_bv, L0_gnn_We, L0_gnn_Wp, L0_gnn_bp, L0_gnn_ln1_g, L0_gnn_ln1_b, L0_gnn_ln2_g, L0_gnn_ln2_b, L0_gnn_W1, L0_gnn_b1, L0_gnn_W2, L0_gnn_b2):
    import jax
    import jax.numpy as jnp

    def _L0_gnn_ref(x, edge_index, edge_attr, Wq, bq, Wk, bk, Wv, bv, We, Wp, bp, ln1_g, ln1_b, ln2_g, ln2_b, W1, b1, W2, b2):
        import math
        import jax, jax.numpy as jnp
        import numpy as np
        N_NODES = 6250
        N_EDGES = 75000
        IN_CH = 64
        HEADS = 2
        C = 64
        HC = HEADS * C
        EDGE_DIM = 32

        def _layernorm(x, g, b, eps=1e-05):
            m = jnp.mean(x, axis=-1, keepdims=True)
            v = jnp.mean(jnp.square(x - m), axis=-1, keepdims=True)
            return (x - m) / jnp.sqrt(v + eps) * g + b
        n = x.shape[0]
        residual = x
        h = _layernorm(x, ln1_g, ln1_b)
        q = (h @ Wq + bq).reshape(n, HEADS, C)
        k = (h @ Wk + bk).reshape(n, HEADS, C)
        v = (h @ Wv + bv).reshape(n, HEADS, C)
        src, tgt = (edge_index[0], edge_index[1])
        e = (edge_attr @ We).reshape(-1, HEADS, C)
        qi = q[tgt]
        kj = k[src] + e
        vj = v[src] + e
        alpha = jnp.sum(qi * kj, axis=-1) / math.sqrt(C)
        amax = jax.ops.segment_max(alpha, tgt, num_segments=n)
        ex = jnp.exp(alpha - amax[tgt])
        den = jax.ops.segment_sum(ex, tgt, num_segments=n)
        a = ex / (den[tgt] + 1e-08)
        agg = jax.ops.segment_sum(a[:, :, None] * vj, tgt, num_segments=n)
        out = agg.reshape(n, HC) @ Wp + bp
        out = out + residual
        res2 = out
        o = _layernorm(out, ln2_g, ln2_b)
        o = jax.nn.gelu(o @ W1 + b1, approximate=False) @ W2 + b2
        return o + res2
    edge_index = jnp.stack([src, dst])
    h = jnp.maximum(_layernorm(x, axis=-1), 0.0)
    x = x + _L0_gnn_ref(h, edge_index, edge_attr_32, L0_gnn_Wq, L0_gnn_bq, L0_gnn_Wk, L0_gnn_bk, L0_gnn_Wv, L0_gnn_bv, L0_gnn_We, L0_gnn_Wp, L0_gnn_bp, L0_gnn_ln1_g, L0_gnn_ln1_b, L0_gnn_ln2_g, L0_gnn_ln2_b, L0_gnn_W1, L0_gnn_b1, L0_gnn_W2, L0_gnn_b2)
    return x

_drawn_inputs = setup_inputs


def setup_inputs(seed=0):
    import zlib

    import numpy as np

    out = dict(_drawn_inputs(seed))
    spreads = {'L0_gnn_bq': (0.0, 0.8),
     'L0_gnn_bk': (0.0, 0.8),
     'L0_gnn_bv': (0.0, 0.1),
     'L0_gnn_bp': (0.0, 0.1),
     'L0_gnn_ln1_g': (1.0, 0.6),
     'L0_gnn_ln1_b': (0.0, 0.54),
     'L0_gnn_ln2_g': (1.0, 0.6),
     'L0_gnn_ln2_b': (0.0, 0.8),
     'L0_gnn_b1': (0.0, 0.553),
     'L0_gnn_b2': (0.0, 0.1)}
    factors = {'L0_gnn_Wq': 5.515, 'L0_gnn_Wk': 6.644}
    for name, (base, spread) in spreads.items():
        noise = np.random.default_rng([zlib.crc32(name.encode()), seed]).standard_normal(out[name].shape)
        drawn = base * np.exp(spread * noise) if base else spread * noise
        out[name] = jnp.asarray(drawn.astype(out[name].dtype))
    for name, factor in factors.items():
        out[name] = (out[name] * factor).astype(out[name].dtype)
    return out
```

```python
import numpy as np
import concourse.bass as bass
from concourse import mybir
from contextlib import ExitStack

F32 = mybir.dt.float32
I32 = mybir.dt.int32
ALU = mybir.AluOpType
ACT = mybir.ActivationFunctionType
X_AXIS = mybir.AxisListType.X
ENG = mybir.EngineType

N, C = 12500, 64
E, CE = 212500, 32
H = 2
Z = C + CE + 1
P = 128
NP, NT = 125, 100
T = 128
K = 32
G = 8
NG = K // G
CHUNKS = -(-E // (K * T))
TILES = CHUNKS * K
JB = TILES // P
PRE = 128
PADDED = PRE + TILES * T + T
LAST_TILES, LAST_ROWS = divmod(E - (TILES - G) * T, T)
R = H * K
NARROW, WIDE = 32, 128
BATCH = 256 // NARROW
SPAN = BATCH // 2 * NARROW
NW = N + WIDE
BIG = 1e30
EPS = 1e-5
PARTS, PT = 4, 25
OT = 4
OGROUPS = NT // OT
FULL_P = 112


def gnn_kernel(nc, x, src, dst, edge_attr, Wq, bq, Wk, bk, Wv, bv, We, Wp, bp,
               ln1_g, ln1_b, ln2_g, ln2_b, W1, b1, W2, b2, out):
    ctx = ExitStack()
    with ctx:
        ctx.enter_context(nc.allow_non_contiguous_dma(reason="weight vectors as columns, tile ends"))

        def sb(name, shape, dt=F32):
            return ctx.enter_context(nc.sbuf_tensor(name, shape, dt))

        def sem(name):
            return ctx.enter_context(nc.semaphore(name))

        table = nc.dram_tensor("table", [N, C], F32).ap()
        h_rows = nc.dram_tensor("h_rows", [N, C], F32).ap()
        dst_pad = nc.dram_tensor("dst_pad", [1, PADDED], I32).ap()
        dst_rows = nc.dram_tensor("dst_rows", [TILES, T], F32).ap()
        src_cols = nc.dram_tensor("src_cols", [P, TILES], I32).ap()
        rel_cols = nc.dram_tensor("rel_cols", [P, TILES], F32).ap()

        acc = sb("acc", [P, H, NW])
        hnT = sb("hnT", [C + 1, NW])
        z = sb("z", [P, 2 * K, Z])
        arena = acc[:, :, :].rearrange("p h n -> p (h n)")
        zflat = z[:, :, :].rearrange("p k z -> p (k z)")

        xs = arena[0:NP, 0:NT * C].rearrange("p (t c) -> p t c", c=C)
        hn = arena[0:NP, NT * C:2 * NT * C].rearrange("p (t c) -> p t c", c=C)
        hs = arena[0:NP, 2 * NT * C:3 * NT * C].rearrange("p (t c) -> p t c", c=C)
        at = 3 * NT * C
        src_i = arena[:, at:at + TILES].bitcast(I32)
        dst_i = arena[:, at + TILES:at + 2 * TILES].bitcast(I32)
        src_f = arena[:, at + 2 * TILES:at + 3 * TILES]
        dst_f = zflat[:, 0:TILES]
        src_t = zflat[:, TILES:2 * TILES].bitcast(I32)
        rel_p = zflat[:, TILES:2 * TILES]
        rel_t = zflat[:, 2 * TILES:3 * TILES]

        ident = sb("ident", [P, P])
        ones = sb("ones", [1, P])
        eps_col = sb("eps_col", [P, 1])
        stat = sb("stat", [P, 6, NT])
        iota = sb("iota", [P, WIDE])
        pad_i = sb("pad_i", [1, PRE], I32)
        flag = sb("flag", [P, 4])
        flag_row = sb("flag_row", [1, P])
        narrow_i = sb("narrow_i", [1, 1], I32)

        zT = sb("zT", [Z, 2, 1024])
        zT_flat = zT[:, :, :].rearrange("z a n -> z (a n)")
        taken = [0]

        def early(rows_, n):
            taken[0] += n
            return zT_flat[0:rows_, taken[0] - n:taken[0]]

        wq, wk, wv = early(C, H * C), early(C, H * C), early(C, H * C)
        we = early(CE, H * C)
        bias = early(1, 3 * H * C).rearrange("a (i n) -> a i n", i=3)
        spread = early(C, Z)
        spread_e = early(CE, Z)
        spread_q = early(C, C + 1)
        unit = early(1, Z + C + 1)
        wqT = early(C, H * (C + 1)).rearrange("c (h n) -> c h n", h=H)
        wkT = early(C, H * Z).rearrange("c (h n) -> c h n", h=H)
        wvT = early(C, H * Z).rearrange("c (h n) -> c h n", h=H)
        assert taken[0] <= 2 * 1024
        wp = sb("wp", [C, H, C])
        cols = sb("cols", [C, 5])
        amat = sb("amat", [C + 1, H, Z])
        vmat = sb("vmat", [Z, H, C + 1])
        w1 = sb("w1", [C, C])
        w2 = sb("w2", [C, C])
        b1c = sb("b1c", [C, 1])
        rows = sb("rows", [P, 2, C])

        idx = sb("idx", [P, 2, K], I32)
        rel = sb("rel", [P, 2, K])
        rel_b = sb("rel_b", [P, K])
        keys = sb("keys", [1, 2, 2 * K + 2], I32)
        keys_b = sb("keys_b", [1, 2 * K + 2], I32)
        drow = sb("drow", [R, 2, T])
        uwin = sb("uwin", [Z, 512])
        prod = sb("prod", [P, 512])
        pick = sb("pick", [P, 256])
        wmat = sb("wmat", [P, 2, 512])
        alpha = sb("alpha", [P, H, K])
        keep = sb("keep", [R, T + 1])
        top = sb("top", [R, T])
        top2 = sb("top2", [R, T])
        far = sb("far", [R, T])
        keep2 = sb("keep2", [1, 2 * K + 1])
        fwd2 = sb("fwd2", [1, H, 2 * K])
        top_ends = sb("top_ends", [1, H, 2 * K])
        carry = sb("carry", [1, H])
        spare = sb("spare", [1, 1])
        gone = sb("gone", [1, H])
        drop = sb("drop", [1, H])
        fade = sb("fade", [1, H])
        wexp = sb("wexp", [P, H, K])

        banks = [ctx.enter_context(nc.psum_tensor(f"bank{i}", [P, 512], F32)) for i in range(8)]
        zt_ps, uw_ps, sc_ps, ag_ps, sn_ps = banks[0:2], banks[2], banks[3:5], banks[5:7], banks[7]

        x_v = x.rearrange("(p t) c -> p t c", t=NT)
        table_v = table.rearrange("(p t) c -> p t c", t=NT)
        h_v = h_rows.rearrange("(p t) c -> p t c", t=NT)
        out_v = out.rearrange("(p t) c -> p t c", t=NT)

        def node_dma(eng, to, frm, signal):
            eng.dma_start(to[0:FULL_P], frm[0:FULL_P]).then_inc(signal, 16)
            eng.dma_start(to[FULL_P:NP], frm[FULL_P:NP]).then_inc(signal, 16)

        x_in = [sem(f"x_in{p}") for p in range(PARTS)]
        edges_in = sem("edges_in")
        weights_in = sem("weights_in")
        w_late = sem("w_late")
        ident_ok = sem("ident_ok")
        ids_pad = sem("ids_pad")
        dve_a = sem("dve_a")
        ln_dve = sem("ln_dve")
        ln_act = sem("ln_act")
        hn_ready = sem("hn_ready")
        h_ready = sem("h_ready")
        table_out = sem("table_out")
        lists_out = sem("lists_out")
        src_out = sem("src_out")
        ids_f = sem("ids_f")
        ids_t = sem("ids_t")
        ids_c = sem("ids_c")
        base_ps = sem("base_ps")
        rel_ok = sem("rel_ok")
        fl_pe = sem("fl_pe")
        fl_dve = sem("fl_dve")

        SEGS = 5
        order = [(s, d - s) for d in range(PARTS + SEGS - 1) for s in range(SEGS) if 0 <= d - s < PARTS]
        act_order = [sp for sp in order if sp[0] < SEGS - 1]
        ln_at = {sp: i + 1 for i, sp in enumerate(act_order)}

        with nc.Block() as block:
            @block.sync
            def _(sp):
                for p in range(PARTS):
                    node_dma(sp, xs[:, p * PT:(p + 1) * PT, :], x_v[:, p * PT:(p + 1) * PT, :], x_in[p])
                for p in range(PARTS):
                    cut = slice(p * PT, (p + 1) * PT)
                    sp.wait_ge(h_ready, p + 1)
                    node_dma(sp, h_v[:, cut, :], hs[:, cut, :], table_out)
                    sp.wait_ge(hn_ready, p + 1)
                    node_dma(sp, table_v[:, cut, :], hn[:, cut, :], table_out)
                sp.wait_ge(table_out, PARTS * 64)

            @block.scalar
            def _(act):
                act.wait_ge(ids_pad, 3)
                full = (JB - 1) * P * T
                rest, odd = divmod(E - full, T)
                for lst, to in ((dst, dst_i), (src, src_i)):
                    v = to.rearrange("p (j e) -> p j e", e=T)
                    act.dma_start(v[:, 0:JB - 1, :], lst[0:full].rearrange("(j p e) -> p j e", p=P, e=T))\
                       .then_inc(edges_in, 16)
                    act.dma_start(v[0:rest, JB - 1, :], lst[full:full + rest * T].rearrange("(p e) -> p e", e=T))\
                       .then_inc(edges_in, 16)
                    act.dma_start(v[rest:rest + 1, JB - 1, 0:odd], lst[full + rest * T:E].rearrange("(a e) -> a e", a=1))\
                       .then_inc(edges_in, 16)
                for w, to in ((Wq, wq), (Wk, wk), (Wv, wv), (We, we)):
                    act.dma_start(to[:, :], w).then_inc(weights_in, 16)
                for i, b in enumerate((bq, bk, bv)):
                    act.dma_start(bias[:, i, :], b.rearrange("(a n) -> a n", a=1)).then_inc(weights_in, 16)
                for i, b in enumerate((ln1_g, ln1_b, ln2_g, ln2_b, b1)):
                    act.dma_start(cols[:, i:i + 1], b.rearrange("(n a) -> n a", a=1)).then_inc(weights_in, 16)
                act.dma_start(wp[:, :, :], Wp.rearrange("(h c) o -> c h o", h=H)).then_inc(weights_in, 16)
                act.dma_start(w1[:, :], W1).then_inc(weights_in, 16)
                act.dma_start(w2[:, :], W2).then_inc(weights_in, 16)
                for i, b in enumerate((bp, b2)):
                    act.dma_start(rows[:, i, :], b.rearrange("(a n) -> a n", a=1).broadcast_to([P, C])).then_inc(weights_in, 16)
                act.wait_ge(edges_in, 96)
                act.dma_start(dst_pad[:, 0:PRE], pad_i[:, :]).then_inc(lists_out, 16)
                act.dma_start(dst_pad[:, PADDED - T:PADDED], pad_i[:, 0:T]).then_inc(lists_out, 16)
                act.dma_start(dst_pad[0, PRE:PRE + TILES * T].rearrange("(j p e) -> p j e", p=P, e=T),
                              dst_i.rearrange("p (j e) -> p j e", e=T)).then_inc(lists_out, 16)
                act.wait_ge(ids_f, 1)
                act.dma_start(dst_rows.rearrange("(j p) e -> p j e", p=P),
                              dst_f.rearrange("p (j e) -> p j e", e=T)).then_inc(lists_out, 16)

                def ln_work(s, p):
                    cut = slice(p * PT, (p + 1) * PT)
                    act.wait_ge(ln_dve, ln_at[s, p])
                    if s in (0, 2):
                        nc.scalar.activation(hn[:, cut, :], xs[:, cut, :], ACT.Square).then_inc(ln_act, 1)
                    else:
                        st = stat[0:NP, 2 * (s // 2) + 1, cut]
                        nc.scalar.activation(st, st, ACT.Sqrt, bias=eps_col[0:NP, :], scale=1.0 / C).then_inc(ln_act, 1)

                done = 0
                act.wait_ge(ids_pad, 4)
                for i, (s, p) in enumerate(act_order):
                    ln_work(s, p)
                    if i % 2 == 1 and done < 8:
                        which, q = divmod(done, 4)
                        n = min(4, JB - 4 * q)
                        act.wait_ge(ids_t, done + 1)
                        to = (src_t, rel_t)[which][:, 4 * q * P:(4 * q + n) * P]
                        nc.scalar.activation(to, banks[done % 4][:, 0:n * P], ACT.Copy).then_inc(ids_c, 1)
                        done += 1
                        if done == 4:
                            act.wait_ge(ids_c, 4)
                            act.dma_start(src_cols, src_t).then_inc(src_out, 16)
                assert done == 8
                act.wait_ge(rel_ok, 1)
                act.dma_start(rel_cols, rel_t).then_inc(lists_out, 16)
                act.wait_ge(lists_out, 80)
                act.wait_ge(src_out, 16)
                act.wait_ge(weights_in, 17 * 16)

            @block.gpsimd
            def _(pool):
                nc.gpsimd.memset(src_i[:, TILES - T:TILES], 0).then_inc(ids_pad, 1)
                nc.gpsimd.memset(dst_i[:, TILES - T:TILES], N).then_inc(ids_pad, 1)
                nc.gpsimd.memset(pad_i[:, :], N).then_inc(ids_pad, 1)
                nc.gpsimd.memset(eps_col[:, :], EPS).then_inc(ids_pad, 1)
                nc.gpsimd.memset(ident[:, :], 0.0).then_inc(ident_ok, 1)
                nc.gpsimd.memset(ones[:, :], 1.0).then_inc(ident_ok, 1)
                pool.wait_ge(ident_ok, 2)
                nc.gpsimd.affine_select(out=ident[:, :], in_=ident[:, :], compare_op=ALU.not_equal, fill=1.0,
                                        base=0, pattern=[[-1, P]], channel_multiplier=1).then_inc(ident_ok, 1)
                nc.gpsimd.iota(iota[:, :], [[1, WIDE]], base=0, channel_multiplier=0,
                               allow_small_or_imprecise_dtypes=True).then_inc(ident_ok, 1)
                nc.gpsimd.memset(hnT[0:C, N:NW], 0.0).then_inc(ident_ok, 1)
                pool.wait_ge(ident_ok, 5)
                nc.gpsimd.memset(hnT[C:C + 1, :], 1.0).then_inc(ident_ok, 1)
                pool.wait_ge(ident_ok, 6)
                nc.gpsimd.memset(spread_e[:, :], 0.0).then_inc(ident_ok, 1)
                nc.gpsimd.memset(unit[:, :], 0.0).then_inc(ident_ok, 1)
                pool.wait_ge(ident_ok, 8)

            @block.tensor
            def _(pe):
                pe.wait_ge(ident_ok, 3)
                for which, lst in enumerate((src_f, dst_f)):
                    pe.wait_ge(ids_f, 2 - which)
                    for q in range(4):
                        n = min(4, JB - 4 * q)
                        if which:
                            pe.wait_ge(ids_c, q + 1)
                        for j in range(4 * q, 4 * q + n):
                            last = nc.tensor.transpose(banks[q][:, (j - 4 * q) * P:(j - 4 * q + 1) * P],
                                                       lst[:, j * P:(j + 1) * P], ident[:, :])
                        last.then_inc(ids_t, 1)
                for q in range(4):
                    pe.wait_ge(ids_c, 8)
                    nc.tensor.matmul(banks[q][:, 0:TILES // 4], ones[0:1, :], rel_t[0:1, q * (TILES // 4):(q + 1) * (TILES // 4)],
                                     start=True, stop=True).then_inc(base_ps, 1)
                pe.wait_ge(fl_dve, 1)
                nc.tensor.transpose(banks[4][0:1, 0:P], flag[:, 0:1], ident[:, :]).then_inc(fl_pe, 1)
                pe.wait_ge(fl_dve, 2)
                nc.tensor.matmul(banks[4][:, P:P + 1], ones[0:1, :], flag_row[0:1, 1:2], start=True, stop=True).then_inc(fl_pe, 1)

            @block.vector
            def _(dve):
                chain = [0]

                def link(ins):
                    chain[0] += 1
                    ins.then_inc(dve_a, 1)
                    dve.wait_ge(dve_a, chain[0])

                dve.wait_ge(edges_in, 96)
                nc.vector.tensor_copy(dst_f, dst_i).then_inc(ids_f, 1)
                nc.vector.tensor_copy(src_f, src_i).then_inc(ids_f, 1)

                def centre(frm, st, cut):
                    link(nc.vector.tensor_reduce(st, frm[:, cut, :], X_AXIS, ALU.add))
                    link(nc.vector.tensor_scalar(st, st, 1.0 / C, None, ALU.mult))
                    nc.vector.tensor_tensor(xs[:, cut, :], frm[:, cut, :], st.unsqueeze(2).broadcast_to([NP, PT, C]),
                                            ALU.subtract).then_inc(ln_dve, 1)

                def segment(s, p):
                    cut = slice(p * PT, (p + 1) * PT)
                    if s == 0:
                        dve.wait_ge(x_in[p], 32)
                        centre(xs, stat[0:NP, 0, cut], cut)
                    elif s in (1, 3):
                        dve.wait_ge(ln_act, ln_at[s - 1, p])
                        nc.vector.tensor_reduce(stat[0:NP, s, cut], hn[:, cut, :], X_AXIS, ALU.add)\
                          .then_inc(ln_dve, 1)
                    elif s == 2:
                        dve.wait_ge(ln_act, ln_at[1, p])
                        inv = stat[0:NP, 4, cut]
                        link(nc.vector.reciprocal(inv, stat[0:NP, 1, cut]))
                        nc.vector.scalar_tensor_tensor(hs[:, cut, :], xs[:, cut, :], 0.0,
                                                       inv.unsqueeze(2).broadcast_to([NP, PT, C]),
                                                       ALU.max, ALU.mult).then_inc(h_ready, 1)
                        dve.wait_ge(h_ready, p + 1)
                        centre(hs, stat[0:NP, 2, cut], cut)
                    else:
                        dve.wait_ge(ln_act, ln_at[3, p])
                        inv = stat[0:NP, 5, cut]
                        link(nc.vector.reciprocal(inv, stat[0:NP, 3, cut]))
                        nc.vector.tensor_tensor(hn[:, cut, :], xs[:, cut, :], inv.unsqueeze(2).broadcast_to([NP, PT, C]),
                                                ALU.mult).then_inc(hn_ready, 1)

                for s, p in order:
                    segment(s, p)
                dve.wait_ge(src_out, 16)
                B = TILES // 4
                for q in range(4):
                    dve.wait_ge(base_ps, q + 1)
                    v = rel_t[:, q * B:(q + 1) * B]
                    pair = banks[q][:, 0:B].rearrange("p (m two) -> p m two", two=2)[:, :, 0:1].broadcast_to([P, B // 2, 2])
                    link(nc.vector.tensor_tensor(rel_p[:, q * B:(q + 1) * B].rearrange("p (m two) -> p m two", two=2),
                                                 v.rearrange("p (m two) -> p m two", two=2), pair, ALU.subtract))
                for q in range(4):
                    v = rel_t[:, q * B:(q + 1) * B]
                    link(nc.vector.tensor_tensor(v, v, banks[q][:, 0:B], ALU.subtract))
                nc.vector.tensor_reduce(flag[:, 0:1], rel_p, X_AXIS, ALU.max).then_inc(fl_dve, 1)
                dve.wait_ge(fl_pe, 1)
                link(nc.vector.tensor_reduce(flag_row[0:1, 0:1], banks[4][0:1, 0:P], X_AXIS, ALU.max))
                nc.vector.tensor_scalar(flag_row[0:1, 1:2], flag_row[0:1, 0:1], float(NARROW - 1), None, ALU.is_le)\
                  .then_inc(fl_dve, 1)
                dve.wait_ge(fl_dve, 2)
                link(nc.vector.tensor_copy(narrow_i[:, :], flag_row[0:1, 1:2]))
                dve.wait_ge(fl_pe, 2)
                link(nc.vector.tensor_copy(flag[:, 1:2], banks[4][:, P:P + 1]))
                link(nc.vector.tensor_tensor(rel_p, rel_p, rel_t, ALU.subtract))
                nc.vector.scalar_tensor_tensor(rel_t, rel_p, flag[:, 1:2], rel_t, ALU.mult, ALU.add).then_inc(rel_ok, 1)
                dve.wait_ge(rel_ok, 1)

        gathered = [sem(f"gathered{i}") for i in range(2 * NG)]
        attrs_in = [sem(f"attrs_in{i}") for i in range(2 * NG)]
        idx_in = [sem(f"idx_in{i}") for i in range(2)]
        meta_in = [sem(f"meta_in{i}") for i in range(2)]
        z_ones = sem("z_ones")
        hn_t = sem("hn_t")
        hn_c = sem("hn_c")
        acc_zero = sem("acc_zero")
        w_dve = sem("w_dve")
        w_pe = sem("w_pe")
        w_act = sem("w_act")
        uw_ready, uw_sb = sem("uw_ready"), sem("uw_sb")
        zt_ready, zt_sb = sem("zt_ready"), sem("zt_sb")
        sc_ready, sc_read, alpha_ready = sem("sc_ready"), sem("sc_read"), sem("alpha_ready")
        wmat_ready, tiles_summed, acc_added = sem("wmat_ready"), sem("tiles_summed"), sem("acc_added")
        alphaT_ready, top_ready, ends_ready = sem("alphaT_ready"), sem("top_ready"), sem("ends_ready")
        ends_top, ends_cols = sem("ends_top"), sem("ends_cols")
        fade_ready, fade_ps, logw_ready, logwT, wexp_ready = (sem("fade_ready"), sem("fade_ps"), sem("logw_ready"),
                                                              sem("logwT"), sem("wexp_ready"))
        drop_ready = sem("drop_ready")
        dve_b = sem("dve_b")
        scan_done = sem("scan_done")

        passed = {nc.tensor: sem("pe_passed"), nc.gpsimd: sem("pool_passed")}

        def wait_apart(eng, signal, value):
            eng.wait_ge(signal, value)
            eng.sem_inc(passed[eng if eng in passed else (nc.tensor if eng.engine == ENG.PE else nc.gpsimd)], 1)

        def slot(par, g):
            return par * NG + g

        def over_chunks(eng, first, body, last):
            c = first
            if c % 2:
                body(c, 1, c // 2)
                c += 1
            pairs = (last - c) // 2
            with eng.Fori(c // 2, c // 2 + pairs) as i:
                body(i * 2, 0, i)
                body(i * 2 + 1, 1, i)
            if c + 2 * pairs < last:
                body(last - 1, (last - 1) % 2, (last - 1) // 2)

        def edge_phase(W, TB, span=None):
            BT = 256 // W
            NB = K // BT
            PB = BT // TB
            ZB = min(4, BT)
            HB = BT // ZB
            UN = H * (span or PB * W)

            def windows(eng, keys_ap, b, n=PB):
                first = 1 + 2 * b * BT
                _, v = nc.values_load_multi_w_load_instructions(
                    keys_ap[0:1, first:first + 2 * TB * (n - 1) + 1:2 * TB], engines=(eng,), min_val=0, max_val=N,
                    skip_runtime_bounds_check_because="dst is a node or the padding's node N")
                return v

            def offset(v, w):
                return nc.s_assert_within(v[w] - v[0], 0, span - W,
                                          skip_runtime_bounds_check_because="every pair of tiles fits a window on this path")

            def pe_scores(pe, c, par, half, b, v):
                if not (isinstance(c, int) and c == 0 and b == 0):
                    pe.wait_ge(uw_sb, c * NB + b)
                width = span or W
                for w, first in enumerate(v):
                    for h in range(H):
                        last = nc.tensor.matmul(uw_ps[0:Z, (w * H + h) * width:(w * H + h + 1) * width], amat[:, h, :],
                                                hnT[:, bass.ds(first, width)], start=True, stop=True)
                last.then_inc(uw_ready, 1)
                if b * BT % G == 0:
                    g = b * BT // G
                    pe.wait_ge(gathered[slot(par, g)], half * (16 * G) + 16 * G)
                    extra = 16 if isinstance(c, int) and c == CHUNKS - 1 and g == NG - 1 else 0
                    pe.wait_ge(attrs_in[slot(par, g)], half * 16 + 16 + extra)
                for j in range(HB):
                    bank = (b * HB + j) % 2
                    if not (isinstance(c, int) and c == 0 and b * HB + j < 2):
                        pe.wait_ge(zt_sb, c * (NB * HB) + (b * HB + j - 1))
                    for i in range(ZB):
                        k = par * K + b * BT + j * ZB + i
                        last = nc.tensor.transpose(zt_ps[bank][0:Z, i * T:(i + 1) * T], z[:, k, :], ident[:, :])
                    last.then_inc(zt_ready, 1)

            def pe_scores_end(pe, c, par, half, b):
                cut = [uwin[:, w * H * W:(w + 1) * H * W] for w in range(PB)]
                if span:
                    v = windows(ENG.PE, keys[:, par, :], b)
                    cut = [uwin[:, 0:H * span].rearrange("z (h n) -> z h n", h=H)
                           [:, :, bass.ds(offset(v, w) if w else 0, W)]
                           for w in range(PB)]
                pe.wait_ge(uw_sb, c * NB + (b + 1))
                if not (isinstance(c, int) and c == 0 and b < 2):
                    pe.wait_ge(sc_read, c * NB + (b - 1))
                for j in range(HB):
                    pe.wait_ge(zt_sb, c * (NB * HB) + (b * HB + j + 1))
                    for i in range(ZB):
                        t = j * ZB + i
                        w = t // TB
                        last = nc.tensor.matmul(sc_ps[b % 2][:, t * H * W:(t + 1) * H * W],
                                                zT[:, b % 2, t * T:(t + 1) * T],
                                                cut[w], start=True, stop=True)
                last.then_inc(sc_ready, 1)

            def pe_sums(pe, c, par, b):
                pe.wait_ge(wmat_ready, c * NB + (b + 1))
                if not (isinstance(c, int) and c == 0 and b < 2):
                    pe.wait_ge(acc_added, c * (NB * PB) + (b - 1) * PB)
                for t in range(BT):
                    w = t // TB
                    last = nc.tensor.matmul(ag_ps[b % 2][0:Z, w * H * W:(w + 1) * H * W], z[:, par * K + b * BT + t, :],
                                            wmat[:, b % 2, t * H * W:(t + 1) * H * W],
                                            start=(t % TB == 0), stop=(t % TB == TB - 1))
                last.then_inc(tiles_summed, BT)

            def pe_scan(pe, c):
                wait_apart(pe, alpha_ready, c * NB + NB)
                if not (isinstance(c, int) and c == 0):
                    wait_apart(pe, wexp_ready, c)
                nc.tensor.transpose(sn_ps[0:R, 0:T], alpha[:, :, :].rearrange("p h k -> p (h k)"), ident[:, :])\
                  .then_inc(alphaT_ready, 1)
                wait_apart(pe, top_ready, c + 1)
                ends = sn_ps[0:1, T:2 * T].rearrange("a (r two) -> a r two", two=2)
                nc.tensor.transpose(ends[:, :, 0], top[:, 0:1], ident[0:R, 0:R])
                nc.tensor.transpose(ends[:, :, 1], top[:, T - 1:T], ident[0:R, 0:R]).then_inc(ends_ready, 1)
                wait_apart(pe, ends_top, c * H + H)
                rows_v = top_ends[:, :, :].rearrange("a h (k two) -> a (h k) two", two=2)
                for j in range(2):
                    last = nc.tensor.matmul(sn_ps[0:R, 2 * T + j:2 * T + j + 1], rows_v[:, :, j], ones[0:1, 0:1],
                                            start=True, stop=True)
                last.then_inc(ends_cols, 1)
                pe.wait_ge(fade_ready, c + 1)
                nc.tensor.matmul(sn_ps[0:Z, 2 * T + 2:2 * T + 4], ones[0:1, 0:Z], fade[0:1, :], start=True, stop=True)\
                  .then_inc(fade_ps, 1)
                wait_apart(pe, logw_ready, c + 1)
                nc.tensor.transpose(sn_ps[:, 2 * T + R:2 * T + 2 * R], top2[:, :], ident[0:R, 0:R]).then_inc(logwT, 1)

            def pe_step(pe, c, par, half, sums=True):
                wait_apart(pe, meta_in[par], half * 64 + 64)
                v = windows(ENG.PE, keys[:, par, :], 0, 1 if span else PB)
                for b in range(NB):
                    pe_scores(pe, c, par, half, b, v)
                    if sums:
                        pe_sums(pe, c - 1, 1 - par, b)
                    if b + 1 < NB:
                        v = windows(ENG.PE, keys[:, par, :], b + 1, 1 if span else PB)
                    pe_scores_end(pe, c, par, half, b)
                pe_scan(pe, c)

            def tensor(pe):
                pe_step(pe, 0, 0, 0, sums=False)
                over_chunks(pe, 1, lambda c, par, half: pe_step(pe, c, par, half), CHUNKS - 1)
                pe_step(pe, CHUNKS - 1, 1, CHUNKS // 2 - 1)
                for b in range(NB):
                    pe_sums(pe, CHUNKS - 1, 1, b)

            def act_step(act, c, par, half):
                for b in range(NB):
                    act.wait_ge(uw_ready, c * NB + (b + 1))
                    if not (isinstance(c, int) and c == 0 and b == 0):
                        act.wait_ge(sc_ready, c * NB + b)
                    nc.scalar.activation(uwin[:, 0:UN], uw_ps[0:Z, 0:UN], ACT.Copy).then_inc(uw_sb, 1)
                    for j in range(HB):
                        act.wait_ge(zt_ready, c * (NB * HB) + (b * HB + j + 1))
                        nc.scalar.activation(zT[:, b % 2, j * ZB * T:(j + 1) * ZB * T], zt_ps[(b * HB + j) % 2][0:Z, 0:ZB * T],
                                             ACT.Copy).then_inc(zt_sb, 1)
                act.wait_ge(drop_ready, c + 1)
                nc.scalar.activation(fade[:, :], drop[:, :], ACT.Exp).then_inc(fade_ready, 1)
                act.wait_ge(logwT, c + 1)
                if not (isinstance(c, int) and c == 0):
                    act.wait_ge(wmat_ready, c * NB)
                nc.scalar.activation(wexp[:, :, :].rearrange("p h k -> p (h k)"), sn_ps[:, 2 * T + R:2 * T + 2 * R],
                                     ACT.Exp).then_inc(wexp_ready, 1)

            def scalar(act):
                act_step(act, 0, 0, 0)
                over_chunks(act, 1, lambda c, par, half: act_step(act, c, par, half), CHUNKS)

            IN_SUMS, IN_SCORES, IN_SCAN = NB, NB, 14
            per_step = IN_SUMS + IN_SCORES + IN_SCAN

            class Own:
                def __init__(self, dve, start):
                    self.dve, self.start, self.n = dve, start, 0

                def link(self, ins):
                    self.n += 1
                    ins.then_inc(dve_b, 1)
                    self.dve.wait_ge(dve_b, self.start + self.n)

            def dve_pick(own, offsets, b):
                own.link(nc.vector.tensor_tensor(
                    pick[:, :].rearrange("p (t w) -> p t w", w=W),
                    iota[:, 0:W].unsqueeze(1).broadcast_to([P, BT, W]),
                    offsets[:, b * BT:(b + 1) * BT].unsqueeze(2).broadcast_to([P, BT, W]), ALU.is_equal))

            def picked():
                return pick[:, :].rearrange("p (t w) -> p t w", w=W).unsqueeze(2).broadcast_to([P, BT, H, W])

            def four(ap):
                return ap.rearrange("p (t h w) -> p t h w", h=H, w=W)

            def dve_weights(dve, own, c, b):
                dve_pick(own, rel_b[:, :], b)
                if b == 0:
                    dve.wait_ge(wexp_ready, c + 1)
                if not (isinstance(c, int) and c == 0 and b < 2):
                    dve.wait_ge(tiles_summed, c * K + (b - 1) * BT)
                w = wexp[:, :, b * BT:(b + 1) * BT].rearrange("p h t -> p t h").unsqueeze(3).broadcast_to([P, BT, H, W])
                nc.vector.tensor_tensor(four(wmat[:, b % 2, :]), picked(), w, ALU.mult).then_inc(wmat_ready, 1)
                dve.wait_ge(wmat_ready, c * NB + (b + 1))

            def dve_add(dve, c, b, v):
                dve.wait_ge(tiles_summed, c * K + (b + 1) * BT)
                for w in range(PB):
                    if not (isinstance(c, int) and c == 0 and b + w == 0):
                        dve.wait_ge(acc_added, c * (NB * PB) + (b * PB + w))
                    a = acc[0:Z, :, bass.ds(v[w], W)]
                    nc.vector.tensor_tensor(a, a, ag_ps[b % 2][0:Z, w * H * W:(w + 1) * H * W]
                                            .rearrange("p (h w) -> p h w", h=H), ALU.add).then_inc(acc_added, 1)

            def dve_scores(dve, own, c, par, half, b):
                if b == 0:
                    dve.wait_ge(meta_in[par], half * 64 + 64)
                dve_pick(own, rel[:, par, :], b)
                dve.wait_ge(sc_ready, c * NB + (b + 1))
                if not (isinstance(c, int) and c == 0 and b == 0):
                    dve.wait_ge(alpha_ready, c * NB + b)
                nc.vector.tensor_tensor(four(prod[:, :]), four(sc_ps[b % 2][:, :]), picked(), ALU.mult).then_inc(sc_read, 1)
                dve.wait_ge(sc_read, c * NB + (b + 1))
                if b == 0 and not (isinstance(c, int) and c == 0):
                    dve.wait_ge(alphaT_ready, c)
                nc.vector.tensor_reduce(alpha[:, :, b * BT:(b + 1) * BT].rearrange("p h t -> p t h"),
                                        four(prod[:, :]), X_AXIS, ALU.add).then_inc(alpha_ready, 1)

            def dve_scan(dve, own, c, par):
                d = drow[:, par, :]
                kk = keys[:, par, :]
                _, open_node = nc.values_load_multi_w_load_instructions(
                    kk[0:1, 0:1], engines=(ENG.DVE,), min_val=0, max_val=N,
                    skip_runtime_bounds_check_because="dst is a node or the padding's node N")
                own.link(nc.vector.tensor_tensor(keep[:, 1:T], d[:, 1:T], d[:, 0:T - 1], ALU.is_equal))
                own.link(nc.vector.tensor_scalar(keep[:, 1:T], keep[:, 1:T], 2 * BIG, -BIG, ALU.mult, ALU.add))
                own.link(nc.vector.tensor_tensor(keep2[:, 0:2 * K], kk[:, 1:2 * K + 1], kk[:, 0:2 * K], ALU.is_equal))
                own.link(nc.vector.tensor_scalar(keep2[:, 0:2 * K], keep2[:, 0:2 * K], 2 * BIG, -BIG, ALU.mult, ALU.add))
                dve.wait_ge(alphaT_ready, c + 1)
                own.link(nc.vector.tensor_tensor_scan(far[:, :], keep[:, 0:T], sn_ps[0:R, 0:T], -BIG, ALU.min, ALU.max))
                nc.vector.tensor_tensor_scan(top[:, T - 1::-1], keep[:, T:0:-1], far[:, T - 1::-1], -BIG, ALU.min, ALU.max)\
                  .then_inc(top_ready, 1)
                dve.wait_ge(ends_ready, c + 1)
                for h in range(H):
                    ins = nc.vector.tensor_tensor_scan(fwd2[:, h, :], keep2[:, 0:2 * K], sn_ps[0:1, T + h * 2 * K:T + (h + 1) * 2 * K],
                                                       carry[:, h:h + 1], ALU.min, ALU.max)
                    own.link(ins)
                for h in range(H):
                    nc.vector.tensor_tensor_scan(top_ends[:, h, ::-1], keep2[:, 2 * K:0:-1], fwd2[:, h, ::-1], -BIG,
                                                 ALU.min, ALU.max).then_inc(ends_top, 1)
                dve.wait_ge(ends_top, c * H + H)
                own.link(nc.vector.scalar_tensor_tensor(gone[:, :], top_ends[:, :, 0], keep2[0:1, 0:1], carry[:, :], ALU.min, ALU.max))
                nc.vector.tensor_tensor(drop[:, :], carry[:, :], gone[:, :], ALU.subtract).then_inc(drop_ready, 1)
                dve.wait_ge(drop_ready, c + 1)
                own.link(nc.vector.tensor_copy(carry[:, :], top_ends[:, :, 2 * K - 1]))
                own.link(nc.vector.tensor_scalar(far[:, :], d, d[:, 0:1], -BIG, ALU.not_equal, ALU.mult))
                dve.wait_ge(ends_cols, c + 1)
                dve.wait_ge(fade_ps, c + 1)
                own.link(nc.vector.scalar_tensor_tensor(top2[:, :], far[:, :], sn_ps[0:R, 2 * T:2 * T + 1], top[:, :], ALU.add, ALU.max))
                own.link(nc.vector.tensor_scalar(far[:, :], d, d[:, T - 1:T], -BIG, ALU.not_equal, ALU.mult))
                own.link(nc.vector.scalar_tensor_tensor(top[:, :], far[:, :], sn_ps[0:R, 2 * T + 1:2 * T + 2], top2[:, :], ALU.add, ALU.max))
                if isinstance(c, int) and c == 0:
                    dve.wait_ge(acc_zero, 1)
                else:
                    dve.wait_ge(acc_added, c * (NB * PB))
                node = acc[0:Z, :, bass.ds(open_node[0], 1)]
                own.link(nc.vector.tensor_tensor(node, node, sn_ps[0:Z, 2 * T + 2:2 * T + 4].unsqueeze(2), ALU.mult))
                nc.vector.tensor_tensor(top2[:, :], sn_ps[0:R, 0:T], top[:, :], ALU.subtract).then_inc(logw_ready, 1)
                nc.vector.tensor_copy(rel_b[:, :], rel[:, par, :])
                nc.vector.tensor_copy(keys_b[:, :], kk).then_inc(scan_done, 1)
                dve.wait_ge(scan_done, c + 1)

            def dve_step(dve, c, par, half, sums=True):
                start = (c - 1) * per_step + (IN_SCORES + IN_SCAN) if sums else 0
                own = Own(dve, start)
                if sums:
                    dve_weights(dve, own, c - 1, 0)
                for b in range(NB):
                    if sums and b + 1 < NB:
                        dve_weights(dve, own, c - 1, b + 1)
                    if sums:
                        dve.wait_ge(scan_done, c)
                        nc.vector.memset(spare[:, :], 0.0)
                        v = windows(ENG.DVE, keys_b[:, :], b)
                    dve_scores(dve, own, c, par, half, b)
                    if sums:
                        dve_add(dve, c - 1, b, v)
                dve_scan(dve, own, c, par)
                assert own.n == (per_step if sums else IN_SCORES + IN_SCAN), own.n

            def vector(dve):
                dve_step(dve, 0, 0, 0, sums=False)
                over_chunks(dve, 1, lambda c, par, half: dve_step(dve, c, par, half), CHUNKS)
                own = Own(dve, (CHUNKS - 1) * per_step + IN_SCORES + IN_SCAN)
                dve_weights(dve, own, CHUNKS - 1, 0)
                for b in range(NB):
                    if b + 1 < NB:
                        dve_weights(dve, own, CHUNKS - 1, b + 1)
                    nc.vector.memset(spare[:, :], 0.0)
                    dve_add(dve, CHUNKS - 1, b, windows(ENG.DVE, keys_b[:, :], b))
                dve.wait_ge(acc_added, CHUNKS * NB * PB)

            return tensor, scalar, vector

        narrow_phase = edge_phase(NARROW, 2, SPAN)
        wide_phase = edge_phase(WIDE, 1)

        def either(engine, builder, which):
            _, v = nc.values_load_multi_w_load_instructions(narrow_i[0:1, 0:1], engines=(engine,), min_val=0, max_val=1,
                                                            skip_runtime_bounds_check_because="a comparison's result")
            with builder.If(v[0] > 0):
                narrow_phase[which](builder)
            with builder.Else():
                wide_phase[which](builder)

        with nc.Block() as block:
            @block.gpsimd
            def _(pool):

                def gather(c, par, half):
                    for g in range(NG):
                        if g == 0:
                            wait_apart(pool, idx_in[par], half * 16 + 16)
                        if not (isinstance(c, int) and c < 2):
                            wait_apart(pool, tiles_summed, (c - 2) * K + (g + 1) * G)
                        for k in range(g * G, (g + 1) * G):
                            pool.indirect_dma_start(z[:, par * K + k, 0:C], None, table,
                                                    bass.IndirectOffsetOnAxis(ap=idx[:, par, k:k + 1], axis=0))\
                                .then_inc(gathered[slot(par, g)], 16)
                gather(0, 0, 0)
                gather(1, 1, 0)
                over_chunks(pool, 2, gather, CHUNKS)

            @block.sync
            def _(sp):
                def attrs(c, par, g):
                    cols_ = z[:, par * K + g * G:par * K + (g + 1) * G, C:C + CE]
                    first = (c * NG + g) * G * T
                    sp.dma_start(cols_, edge_attr[bass.ds(first, G * T), :].rearrange("(k p) f -> p k f", p=T))\
                      .then_inc(attrs_in[slot(par, g)], 16)

                def loads(c, par, half, last=False):
                    early = isinstance(c, int) and c < 2
                    if not early:
                        for g in range(NG):
                            sp.wait_ge(gathered[slot(par, g)], half * (16 * G))
                    sp.dma_start(idx[:, par, :], src_cols[:, bass.ds(c * K, K)]).then_inc(idx_in[par], 16)
                    if not early:
                        sp.wait_ge(scan_done, c - 1)
                    sp.dma_start(rel[:, par, :], rel_cols[:, bass.ds(c * K, K)]).then_inc(meta_in[par], 16)
                    ends = dst_pad[0, bass.ds(c * (K * T) + (PRE - 1), (K + 1) * T)].rearrange("(k e) -> k e", e=T)[:, 0:2]
                    sp.dma_start(keys[:, par, :].rearrange("a (k two) -> a k two", two=2), ends.unsqueeze(0))\
                      .then_inc(meta_in[par], 16)
                    for h in range(H):
                        sp.dma_start(drow[h * K:(h + 1) * K, par, :], dst_rows[bass.ds(c * K, K), :]).then_inc(meta_in[par], 16)
                    for g in range(NG):
                        if not early:
                            sp.wait_ge(tiles_summed, (c - 2) * K + (g + 1) * G)
                        if last and g == NG - 1:
                            k0, e0 = par * K + g * G, (TILES - G) * T
                            sp.dma_start(z[:, k0:k0 + LAST_TILES, C:C + CE],
                                         edge_attr[e0:e0 + LAST_TILES * T, :].rearrange("(k p) f -> p k f", p=T))\
                              .then_inc(attrs_in[slot(par, g)], 16)
                            sp.dma_start(z[0:LAST_ROWS, k0 + LAST_TILES, C:C + CE], edge_attr[e0 + LAST_TILES * T:E, :])\
                              .then_inc(attrs_in[slot(par, g)], 16)
                        else:
                            attrs(c, par, g)
                loads(0, 0, 0)
                loads(1, 1, 0)
                over_chunks(sp, 2, lambda c, par, half: loads(c, par, half), CHUNKS - 2)
                loads(CHUNKS - 2, 0, CHUNKS // 2 - 1)
                loads(CHUNKS - 1, 1, CHUNKS // 2 - 1, last=True)

            @block.tensor
            def _(pe):
                for q in range(NT // OT):
                    if q >= 2:
                        pe.wait_ge(hn_c, q - 1)
                    for t in range(OT):
                        last = nc.tensor.transpose(zt_ps[q % 2][0:C, t * NP:(t + 1) * NP], hn[:, q * OT + t, :], ident[0:NP, 0:NP])
                    last.then_inc(hn_t, 1)
                pe.wait_ge(w_dve, 1)
                uz, uh = unit[:, 0:Z], unit[:, Z:Z + C + 1]
                for i, (w, last_row) in enumerate(((wq, 0), (wk, 1), (wv, 2))):
                    n = C + 1 if i == 0 else Z
                    for h in range(H):
                        o = banks[3 + i][0:C, h * 128:h * 128 + n]
                        hc = slice(h * C, (h + 1) * C)
                        nc.tensor.matmul(o, w[:, hc], spread_q[:, :] if i == 0 else spread[:, :], start=True, stop=False)
                        if i:
                            nc.tensor.matmul(o, we[:, hc], spread_e[:, :], start=False, stop=False)
                        last = nc.tensor.matmul(o, bias[:, i, hc], uh if i == 0 else uz, start=False, stop=True)
                    last.then_inc(w_pe, 1)
                pe.wait_ge(w_act, 3)
                for h in range(H):
                    last = nc.tensor.matmul(banks[6][0:C + 1, h * 128:h * 128 + Z], wqT[:, h, :], wkT[:, h, :], start=True, stop=True)
                last.then_inc(w_pe, 1)
                for h in range(H):
                    last = nc.tensor.matmul(banks[7][0:Z, h * 128:h * 128 + C], wvT[:, h, :], wp[:, h, :], start=True, stop=True)
                last.then_inc(w_pe, 1)
                nc.tensor.matmul(banks[2][0:C, 0:1], w1[:, :], cols[:, 3:4], start=True, stop=True).then_inc(w_pe, 1)
                pe.wait_ge(w_act, 5)
                pe.wait_ge(hn_c, NT // OT)
                pe.wait_ge(w_dve, 2)
                pe.wait_ge(z_ones, 1)
                either(ENG.PE, pe, 0)

            @block.scalar
            def _(act):
                def columns(q):
                    act.wait_ge(hn_t, q + 1)
                    v = hnT[0:C, 0:N].rearrange("c (p t) -> c t p", t=NT)[:, q * OT:(q + 1) * OT, :]
                    nc.scalar.activation(v, zt_ps[q % 2][0:C, 0:OT * NP].rearrange("c (t p) -> c t p", p=NP), ACT.Copy)\
                      .then_inc(hn_c, 1)
                for q in range(NT // OT):
                    columns(q)
                for i, (w, n) in enumerate(((wqT, C + 1), (wkT, Z), (wvT, Z))):
                    act.wait_ge(w_pe, i + 1)
                    nc.scalar.activation(w[:, :, :], banks[3 + i][0:C, 0:256].rearrange("c (h n) -> c h n", h=H)[:, :, 0:n],
                                         ACT.Copy).then_inc(w_act, 1)
                act.wait_ge(w_pe, 4)
                nc.scalar.activation(amat[:, :, :], banks[6][0:C + 1, 0:256].rearrange("c (h n) -> c h n", h=H)[:, :, 0:Z],
                                     ACT.Copy, scale=1.0 / np.sqrt(C).item()).then_inc(w_act, 1)
                act.wait_ge(w_pe, 5)
                nc.scalar.activation(vmat[:, :, 0:C], banks[7][0:Z, 0:256].rearrange("c (h n) -> c h n", h=H)[:, :, 0:C],
                                     ACT.Copy).then_inc(w_act, 1)
                either(ENG.Activation, act, 1)

            @block.vector
            def _(dve):
                k = [0]

                def link(ins):
                    k[0] += 1
                    ins.then_inc(w_late, 1)
                    dve.wait_ge(w_late, k[0])
                nc.vector.memset(z[:, :, Z - 1:Z], 1.0).then_inc(z_ones, 1)
                link(nc.vector.memset(spread[:, :], 0.0))
                g, b = cols[:, 0:1], cols[:, 1:2]
                link(nc.vector.tensor_scalar(spread[:, 0:C], ident[0:C, 0:C], g, None, ALU.mult))
                link(nc.vector.tensor_copy(spread[:, Z - 1:Z], b))
                link(nc.vector.tensor_scalar(spread_q[:, 0:C], ident[0:C, 0:C], g, None, ALU.mult))
                link(nc.vector.tensor_copy(spread_q[:, C:C + 1], b))
                link(nc.vector.tensor_copy(spread_e[:, C:C + CE], ident[0:CE, 0:CE]))
                link(nc.vector.memset(unit[:, Z - 1:Z], 1.0))
                nc.vector.memset(unit[:, Z + C:Z + C + 1], 1.0).then_inc(w_dve, 1)
                link(nc.vector.memset(keep[:, :], -BIG))
                link(nc.vector.memset(keep2[:, :], -BIG))
                link(nc.vector.memset(carry[:, :], 0.0))
                link(nc.vector.tensor_copy(vmat[:, :, C:C + 1].rearrange("z h a -> z (h a)"),
                                           ident[0:Z, Z - 1:Z].broadcast_to([Z, H])))
                dve.wait_ge(w_pe, 6)
                link(nc.vector.tensor_tensor(b1c[:, :], banks[2][0:C, 0:1], cols[:, 4:5], ALU.add))
                nc.vector.tensor_scalar(w1[:, :], w1[:, :], cols[:, 2:3], None, ALU.mult).then_inc(w_dve, 1)
                dve.wait_ge(w_dve, 2)
                dve.wait_ge(hn_c, NT // OT)
                nc.vector.memset(acc[0:Z, :, :], 0.0).then_inc(acc_zero, 1)
                either(ENG.DVE, dve, 2)

        at = [0]

        def room(n, shape_to, np_=NP):
            v = zflat[0:np_, at[0]:at[0] + n]
            at[0] += n
            return v.rearrange(*shape_to[0:1], **shape_to[1])

        tc_ = ("p (t c) -> p t c", dict(c=C))
        GS = OT * C
        st = [room(H * OT * NP, ("z (h t p) -> z h t p", dict(h=H, t=OT)), Z) for _ in range(2)]
        hb = [room(GS, tc_) for _ in range(2)]
        xb = [room(GS, tc_) for _ in range(2)]
        oo = [room(GS, tc_) for _ in range(2)]
        ob = [room(GS, tc_) for _ in range(2)]
        assert at[0] <= 2 * K * Z
        oc = [prod[0:NP, i * GS:(i + 1) * GS].rearrange("p (t c) -> p t c", c=C) for i in range(2)]
        osq = [wmat[0:NP, 0, i * GS:(i + 1) * GS].rearrange("p (t c) -> p t c", c=C) for i in range(2)]
        fin = [wmat[0:NP, 1, i * GS:(i + 1) * GS].rearrange("p (t c) -> p t c", c=C) for i in range(2)]
        oT = [zT[0:C, 0, i * 512:i * 512 + OT * NP] for i in range(2)]
        hT = [zT[0:C, 1, i * 512:i * 512 + OT * NP] for i in range(2)]
        den = [stat[0:NP, 0:H, i * OT:(i + 1) * OT] for i in range(2)]
        den_r = [stat[0:NP, 2:2 + H, i * OT:(i + 1) * OT] for i in range(2)]
        mean = [stat[0:NP, 4, i * OT:(i + 1) * OT] for i in range(2)]
        var = [stat[0:NP, 5, i * OT:(i + 1) * OT] for i in range(2)]
        inv = [stat[0:NP, 4, 16 + i * OT:16 + (i + 1) * OT] for i in range(2)]

        hx_in = [sem(f"hx_in{i}") for i in range(2)]
        out_done = [sem(f"out_done{i}") for i in range(2)]
        st_ready, pr_ready, pr_read = sem("st_ready"), sem("pr_ready"), sem("pr_read")
        hbp_ready, xb_ready, o_ready, ox_ready = sem("hbp_ready"), sem("xb_ready"), sem("o_ready"), sem("ox_ready")
        oc_ready, sq_ready, var_ready, sd_ready, norm_ready = (sem("oc_ready"), sem("sq_ready"), sem("var_ready"),
                                                               sem("sd_ready"), sem("norm_ready"))
        oT_ps, oT_sb, hid_ps, hid_sb, y_ps, fin_ready = (sem("oT_ps"), sem("oT_sb"), sem("hid_ps"), sem("hid_sb"),
                                                         sem("y_ps"), sem("fin_ready"))
        dve_c = sem("dve_c")
        LINKS = 7

        with nc.Block() as block:
            @block.sync
            def _(sp):
                def load(g, s):
                    for v, to in ((h_v, hb[s]), (x_v, xb[s])):
                        node_dma(sp, to, v[:, bass.ds(g * OT, OT), :], hx_in[s])

                def store(g, s):
                    sp.wait_ge(fin_ready, g + 1)
                    node_dma(sp, out_v[:, bass.ds(g * OT, OT), :], fin[s], out_done[s])

                load(0, 0)
                load(1, 1)
                with sp.Fori(0, OGROUPS // 2 - 1) as i:
                    for s in range(2):
                        sp.wait_ge(ox_ready, i * 2 + (s + 1))
                        load(i * 2 + (s + 2), s)
                        store(i * 2 + s, s)
                sp.wait_ge(ox_ready, OGROUPS - 2)
                load(OGROUPS - 1, 0)
                store(OGROUPS - 3, 0)
                store(OGROUPS - 2, 1)
                store(OGROUPS - 1, 0)
                sp.wait_ge(out_done[0], (OGROUPS + 1) // 2 * 32)
                sp.wait_ge(out_done[1], OGROUPS // 2 * 32)

            @block.scalar
            def _(act):
                def stage(g, s, i):
                    if not isinstance(g, int) or g > 1:
                        act.wait_ge(pr_ready, g - 1)
                    v = acc[0:Z, :, 0:N].rearrange("z h (p t) -> z h t p", t=NT)[:, :, bass.ds(g * OT, OT), :]
                    for h in range(H):
                        last = nc.scalar.activation(st[s][:, h], v[:, h], ACT.Copy)
                        last.then_inc(st_ready, 1)

                def rest(g, s, i):
                    act.wait_ge(oc_ready, g + 1)
                    nc.scalar.activation(osq[s], oc[s], ACT.Square).then_inc(sq_ready, 1)
                    act.wait_ge(var_ready, g + 1)
                    nc.scalar.activation(var[s], var[s], ACT.Sqrt, bias=eps_col[0:NP, :], scale=1.0 / C).then_inc(sd_ready, 1)
                    act.wait_ge(oT_ps, g + 1)
                    nc.scalar.activation(oT[s], banks[4][0:C, 0:OT * NP], ACT.Copy).then_inc(oT_sb, 1)
                    act.wait_ge(hid_ps, g + 1)
                    nc.scalar.activation(hT[s], banks[5][0:C, 0:OT * NP], ACT.Gelu, bias=b1c[:, :]).then_inc(hid_sb, 1)

                stage(0, 0, 0)
                stage(1, 1, 0)
                rest(0, 0, 0)
                with act.Fori(0, OGROUPS // 2 - 1) as i:
                    stage(i * 2 + 2, 0, i)
                    rest(i * 2 + 1, 1, i)
                    stage(i * 2 + 3, 1, i)
                    rest(i * 2 + 2, 0, i)
                stage(OGROUPS - 1, 0, 0)
                rest(OGROUPS - 2, 1, 0)
                rest(OGROUPS - 1, 0, 0)

            @block.gpsimd
            def _(pool):
                def body(g, s, i):
                    pool.wait_ge(hx_in[s], i * 64 + 64)
                    nc.gpsimd.tensor_tensor(hb[s], hb[s], rows[0:NP, 0, :].unsqueeze(1).broadcast_to([NP, OT, C]), ALU.add)\
                      .then_inc(hbp_ready, 1)
                    nc.gpsimd.tensor_tensor(xb[s], xb[s], rows[0:NP, 1, :].unsqueeze(1).broadcast_to([NP, OT, C]), ALU.add)\
                      .then_inc(xb_ready, 1)
                    pool.wait_ge(o_ready, g + 1)
                    pool.wait_ge(xb_ready, g + 1)
                    if not isinstance(g, int) or g > 1:
                        pool.wait_ge(fin_ready, g - 1)
                    nc.gpsimd.tensor_tensor(ob[s], oo[s], xb[s], ALU.add).then_inc(ox_ready, 1)
                body(0, 0, 0)
                body(1, 1, 0)
                with pool.Fori(1, OGROUPS // 2) as i:
                    body(i * 2, 0, i)
                    body(i * 2 + 1, 1, i)
                body(OGROUPS - 1, 0, OGROUPS // 2)

            @block.tensor
            def _(pe):
                def project(g, s):
                    pe.wait_ge(st_ready, g * H + H)
                    if not (isinstance(g, int) and g < 2):
                        pe.wait_ge(pr_read, g * H - H)
                    for h in range(H):
                        for t in range(OT):
                            last = nc.tensor.matmul(banks[2 * s + h][0:NP, t * (C + 1):(t + 1) * (C + 1)], st[s][:, h, t, :], vmat[:, h, :],
                                                    start=True, stop=True)
                    last.then_inc(pr_ready, 1)

                def rest(g, s):
                    wait_apart(pe, norm_ready, g + 1)
                    if not (isinstance(g, int) and g == 0):
                        wait_apart(pe, oT_sb, g)
                    for t in range(OT):
                        last = nc.tensor.transpose(banks[4][0:C, t * NP:(t + 1) * NP], oc[s][:, t, :], ident[0:NP, 0:NP])
                    last.then_inc(oT_ps, 1)
                    wait_apart(pe, oT_sb, g + 1)
                    if not (isinstance(g, int) and g == 0):
                        wait_apart(pe, hid_sb, g)
                    nc.tensor.matmul(banks[5][0:C, 0:OT * NP], w1[:, :], oT[s], start=True, stop=True).then_inc(hid_ps, 1)
                    pe.wait_ge(hid_sb, g + 1)
                    if not (isinstance(g, int) and g < 2):
                        pe.wait_ge(fin_ready, g - 1)
                    for t in range(OT):
                        last = nc.tensor.matmul(banks[6 + s][0:NP, t * C:(t + 1) * C], hT[s][:, t * NP:(t + 1) * NP], w2[:, :],
                                                start=True, stop=True)
                    last.then_inc(y_ps, 1)
                project(0, 0)
                project(1, 1)
                rest(0, 0)
                with pe.Fori(0, OGROUPS // 2 - 1) as i:
                    project(i * 2 + 2, 0)
                    rest(i * 2 + 1, 1)
                    project(i * 2 + 3, 1)
                    rest(i * 2 + 2, 0)
                project(OGROUPS - 1, 0)
                rest(OGROUPS - 2, 1)
                rest(OGROUPS - 1, 0)

            @block.vector
            def _(dve):
                def body(g, s, i):
                    n = [0]

                    def link(ins):
                        n[0] += 1
                        ins.then_inc(dve_c, 1)
                        dve.wait_ge(dve_c, g * LINKS + n[0])
                    dve.wait_ge(pr_ready, g + 1)
                    pr = [banks[2 * s + h][0:NP, 0:OT * (C + 1)].rearrange("p (t c) -> p t c", c=C + 1) for h in range(H)]
                    for h in range(H):
                        link(nc.vector.tensor_scalar(den[s][:, h, :], pr[h][:, :, C], 1e-8, None, ALU.add))
                    link(nc.vector.reciprocal(den_r[s], den[s]))
                    if not (isinstance(g, int) and g < 2):
                        dve.wait_ge(ox_ready, g - 1)
                        dve.wait_ge(oT_ps, g - 1)
                    for h, to in enumerate((oo[s], oc[s])):
                        nc.vector.tensor_tensor(to, pr[h][:, :, 0:C], den_r[s][:, h, :].unsqueeze(2).broadcast_to([NP, OT, C]),
                                                ALU.mult).then_inc(pr_read, 1)
                    dve.wait_ge(pr_read, g * H + H)
                    link(nc.vector.tensor_tensor(oo[s], oo[s], oc[s], ALU.add))
                    dve.wait_ge(hbp_ready, g + 1)
                    nc.vector.tensor_tensor(oo[s], oo[s], hb[s], ALU.add).then_inc(o_ready, 1)
                    dve.wait_ge(o_ready, g + 1)
                    link(nc.vector.tensor_reduce(mean[s], oo[s], X_AXIS, ALU.add))
                    link(nc.vector.tensor_scalar(mean[s], mean[s], 1.0 / C, None, ALU.mult))
                    nc.vector.tensor_tensor(oc[s], oo[s], mean[s].unsqueeze(2).broadcast_to([NP, OT, C]), ALU.subtract)\
                      .then_inc(oc_ready, 1)
                    dve.wait_ge(sq_ready, g + 1)
                    nc.vector.tensor_reduce(var[s], osq[s], X_AXIS, ALU.add).then_inc(var_ready, 1)
                    dve.wait_ge(sd_ready, g + 1)
                    link(nc.vector.reciprocal(inv[s], var[s]))
                    nc.vector.tensor_tensor(oc[s], oc[s], inv[s].unsqueeze(2).broadcast_to([NP, OT, C]), ALU.mult)\
                      .then_inc(norm_ready, 1)
                    assert n[0] == LINKS, n[0]

                def finish(g, s, i):
                    dve.wait_ge(y_ps, g + 1)
                    dve.wait_ge(ox_ready, g + 1)
                    if not (isinstance(g, int) and g < 2):
                        dve.wait_ge(out_done[s], i * 32)
                    nc.vector.tensor_tensor(fin[s], banks[6 + s][0:NP, 0:OT * C].rearrange("p (t c) -> p t c", c=C), ob[s],
                                            ALU.add).then_inc(fin_ready, 1)
                body(0, 0, 0)
                body(1, 1, 0)
                finish(0, 0, 0)
                body(2, 0, 1)
                finish(1, 1, 0)
                with dve.Fori(1, OGROUPS // 2) as i:
                    body(i * 2 + 1, 1, i)
                    finish(i * 2, 0, i)
                    body(i * 2 + 2, 0, i)
                    finish(i * 2 + 1, 1, i)
                finish(OGROUPS - 1, 0, OGROUPS // 2)

    return nc


_INS = ["x", "src", "dst", "edge_attr_32"] + [
    "L0_gnn_" + n for n in ("Wq", "bq", "Wk", "bk", "Wv", "bv", "We", "Wp", "bp", "ln1_g", "ln1_b", "ln2_g", "ln2_b",
                            "W1", "b1", "W2", "b2")]


def kernel(**inputs):
    import concourse.bacc as _bacc
    from concourse.bass_utils import run_bass_kernel_spmd as _run

    nc = _bacc.Bacc("TRN2", target_bir_lowering=False, num_devices=1)
    arrays, args = {}, []
    for name in _INS:
        a = np.ascontiguousarray(inputs[name])
        arrays[f"in_{name}"] = a
        args.append(nc.dram_tensor(f"in_{name}", a.shape, mybir.dt.from_np(a.dtype), kind="ExternalInput").ap())
    out = nc.dram_tensor("out_0", (N, C), F32, kind="ExternalOutput").ap()
    gnn_kernel(nc, *args, out)
    return _run(nc, [arrays], core_ids=[0]).results[0]["out_0"]
```

```python
import numpy as np
import concourse.bass as bass
from concourse import mybir
from contextlib import ExitStack

F32 = mybir.dt.float32
I32 = mybir.dt.int32
ALU = mybir.AluOpType
ACT = mybir.ActivationFunctionType
X_AXIS = mybir.AxisListType.X
ENG = mybir.EngineType

N, C = 12500, 64
E, CE = 212500, 32
H = 2
Z = C + CE + 1
P = 128
NP, NT = 125, 100
T = 128
K = 32
G = 8
NG = K // G
CHUNKS = -(-E // (K * T))
TILES = CHUNKS * K
JB = TILES // P
PRE = 128
PADDED = PRE + TILES * T + T
LAST_TILES, LAST_ROWS = divmod(E - (TILES - G) * T, T)
R = H * K
NARROW, WIDE = 32, 128
BATCH = 256 // NARROW
SPAN = BATCH // 2 * NARROW
NW = N + WIDE
BIG = 1e30
EPS = 1e-5
PARTS, PT = 4, 25
OT = 4
OGROUPS = NT // OT
FULL_P = 112


def gnn_kernel(nc, x, src, dst, edge_attr, Wq, bq, Wk, bk, Wv, bv, We, Wp, bp,
               ln1_g, ln1_b, ln2_g, ln2_b, W1, b1, W2, b2, out):
    ctx = ExitStack()
    with ctx:
        ctx.enter_context(nc.allow_non_contiguous_dma(reason="weight vectors as columns, tile ends"))

        def sb(name, shape, dt=F32):
            return ctx.enter_context(nc.sbuf_tensor(name, shape, dt))

        def sem(name):
            return ctx.enter_context(nc.semaphore(name))

        table = nc.dram_tensor("table", [N, C], F32).ap()
        h_rows = nc.dram_tensor("h_rows", [N, C], F32).ap()
        dst_pad = nc.dram_tensor("dst_pad", [1, PADDED], I32).ap()
        dst_rows = nc.dram_tensor("dst_rows", [TILES, T], F32).ap()
        src_cols = nc.dram_tensor("src_cols", [P, TILES], I32).ap()
        rel_cols = nc.dram_tensor("rel_cols", [P, TILES], F32).ap()

        acc = sb("acc", [P, H, NW])
        node_room = sb("node_room", [P, 2 * NT * C])
        hnT = node_room[0:C + 1, 0:NW]
        z = sb("z", [P, 2 * K, Z])
        arena = acc[:, :, :].rearrange("p h n -> p (h n)")
        zflat = z[:, :, :].rearrange("p k z -> p (k z)")

        xs = arena[0:NP, 0:NT * C].rearrange("p (t c) -> p t c", c=C)
        hn = arena[0:NP, NT * C:2 * NT * C].rearrange("p (t c) -> p t c", c=C)
        hs = arena[0:NP, 2 * NT * C:3 * NT * C].rearrange("p (t c) -> p t c", c=C)
        at = 3 * NT * C
        src_i = arena[:, at:at + TILES].bitcast(I32)
        dst_i = arena[:, at + TILES:at + 2 * TILES].bitcast(I32)
        src_f = arena[:, at + 2 * TILES:at + 3 * TILES]
        dst_f = zflat[:, 0:TILES]
        src_t = src_i
        rel_t = arena[:, at + TILES:at + 2 * TILES]
        rel_p = src_f

        ident = sb("ident", [P, P])
        ones = sb("ones", [1, P])
        eps_col = sb("eps_col", [P, 1])
        stat = sb("stat", [P, 6, NT])
        iota = sb("iota", [P, WIDE])
        pad_i = sb("pad_i", [1, PRE], I32)
        flag = sb("flag", [P, 4])
        flag_row = sb("flag_row", [1, P])
        narrow_i = sb("narrow_i", [1, 1], I32)

        zT = sb("zT", [Z, 2, 1024])
        zT_flat = zT[:, :, :].rearrange("z a n -> z (a n)")
        taken = [0]

        def early(rows_, n):
            taken[0] += n
            return zT_flat[0:rows_, taken[0] - n:taken[0]]

        wq, wk, wv = early(C, H * C), early(C, H * C), early(C, H * C)
        we = early(CE, H * C)
        bias = early(1, 3 * H * C).rearrange("a (i n) -> a i n", i=3)
        spread = early(C, Z)
        spread_e = early(CE, Z)
        spread_q = early(C, C + 1)
        unit = early(1, Z + C + 1)
        wqT = early(C, H * (C + 1)).rearrange("c (h n) -> c h n", h=H)
        wkT = early(C, H * Z).rearrange("c (h n) -> c h n", h=H)
        wvT = early(C, H * Z).rearrange("c (h n) -> c h n", h=H)
        assert taken[0] <= 2 * 1024
        wp = sb("wp", [C, H, C])
        cols = sb("cols", [C, 5])
        amat = sb("amat", [C + 1, H, Z])
        vmat = sb("vmat", [Z, H, C + 1])
        w1 = sb("w1", [C, C])
        w2 = sb("w2", [C, C])
        b1c = sb("b1c", [C, 1])
        rows = sb("rows", [P, 2, C])

        idx = sb("idx", [P, 2, K], I32)
        rel = sb("rel", [P, 2, K])
        rel_b = sb("rel_b", [P, K])
        keys = sb("keys", [1, 2, 2 * K + 2], I32)
        keys_b = sb("keys_b", [1, 2 * K + 2], I32)
        drow = sb("drow", [R, 2, T])
        uwin = sb("uwin", [Z, 512])
        prod = sb("prod", [P, 512])
        pick = sb("pick", [P, 256])
        wmat = sb("wmat", [P, 2, 512])
        alpha = sb("alpha", [P, H, K])
        keep = sb("keep", [R, T + 1])
        top = sb("top", [R, T])
        top2 = sb("top2", [R, T])
        far = sb("far", [R, T])
        keep2 = sb("keep2", [1, 2 * K + 1])
        fwd2 = sb("fwd2", [1, H, 2 * K])
        top_ends = sb("top_ends", [1, H, 2 * K])
        carry = sb("carry", [1, H])
        spare = sb("spare", [1, 1])
        gone = sb("gone", [1, H])
        drop = sb("drop", [1, H])
        fade = sb("fade", [1, H])
        wexp = sb("wexp", [P, H, K])

        banks = [ctx.enter_context(nc.psum_tensor(f"bank{i}", [P, 512], F32)) for i in range(8)]
        zt_ps, uw_ps, sc_ps, ag_ps, sn_ps = banks[0:2], banks[2], banks[3:5], banks[5:7], banks[7]
        hn_ps = banks[0:2] + banks[6:8]

        x_v = x.rearrange("(p t) c -> p t c", t=NT)
        table_v = table.rearrange("(p t) c -> p t c", t=NT)
        h_v = h_rows.rearrange("(p t) c -> p t c", t=NT)
        out_v = out.rearrange("(p t) c -> p t c", t=NT)

        def node_dma(eng, to, frm, signal):
            eng.dma_start(to[0:FULL_P], frm[0:FULL_P]).then_inc(signal, 16)
            eng.dma_start(to[FULL_P:NP], frm[FULL_P:NP]).then_inc(signal, 16)

        x_in = [sem(f"x_in{p}") for p in range(PARTS)]
        edges_in = sem("edges_in")
        weights_in = sem("weights_in")
        w_late = sem("w_late")
        ident_ok = sem("ident_ok")
        ids_pad = sem("ids_pad")
        dve_a = sem("dve_a")
        ln_dve = sem("ln_dve")
        ln_act = sem("ln_act")
        mean_ready, inv_ok, pool_ln = sem("mean_ready"), sem("inv_ok"), sem("pool_ln")
        hn_ready = sem("hn_ready")
        hn_last = sem("hn_last")
        h_ready = sem("h_ready")
        table_out = sem("table_out")
        lists_out = sem("lists_out")
        src_out = sem("src_out")
        ids_f = sem("ids_f")
        ids_t = sem("ids_t")
        ids_c = sem("ids_c")
        base_ps = sem("base_ps")
        rel_ok = sem("rel_ok")
        stage1_done = sem("stage1_done")
        idx_in = [sem(f"idx_in{i}") for i in range(2)]
        fl_pe = sem("fl_pe")
        fl_dve = sem("fl_dve")

        SEGS = 5
        order = [(s, d - s) for d in range(PARTS + SEGS - 1) for s in range(SEGS) if 0 <= d - s < PARTS]
        act_order = [sp for sp in order if sp[0] < SEGS - 1]
        ln_at = {sp: i + 1 for i, sp in enumerate(act_order)}

        def sync_1(sp):
            for p in range(PARTS):
                node_dma(sp, xs[:, p * PT:(p + 1) * PT, :], x_v[:, p * PT:(p + 1) * PT, :], x_in[p])
            for p in range(PARTS):
                cut = slice(p * PT, (p + 1) * PT)
                sp.wait_ge(h_ready, p + 1)
                node_dma(sp, h_v[:, cut, :], hs[:, cut, :], table_out)
            sp.wait_ge(src_out, 16)
            for c in range(2):
                sp.dma_start(idx[:, c, :], src_cols[:, c * K:(c + 1) * K]).then_inc(idx_in[c], 16)
            for p in (*range(PARTS - 2), PARTS - 1, PARTS - 2):
                cut = slice(p * PT, (p + 1) * PT)
                if p < PARTS - 1:
                    sp.wait_ge(hn_ready, p + 1)
                else:
                    sp.wait_ge(hn_last, 1)
                node_dma(sp, table_v[:, cut, :], hn[:, cut, :], table_out)
            sp.wait_ge(table_out, PARTS * 64)

        def scalar_1(act):
            act.wait_ge(ids_pad, 3)
            full = (JB - 1) * P * T
            rest, odd = divmod(E - full, T)
            for lst, to in ((dst, dst_i), (src, src_i)):
                v = to.rearrange("p (j e) -> p j e", e=T)
                act.dma_start(v[:, 0:JB - 1, :], lst[0:full].rearrange("(j p e) -> p j e", p=P, e=T))\
                   .then_inc(edges_in, 16)
                act.dma_start(v[0:rest, JB - 1, :], lst[full:full + rest * T].rearrange("(p e) -> p e", e=T))\
                   .then_inc(edges_in, 16)
                act.dma_start(v[rest:rest + 1, JB - 1, 0:odd], lst[full + rest * T:E].rearrange("(a e) -> a e", a=1))\
                   .then_inc(edges_in, 16)
            for w, to in ((Wq, wq), (Wk, wk), (Wv, wv), (We, we)):
                act.dma_start(to[:, :], w).then_inc(weights_in, 16)
            for i, b in enumerate((bq, bk, bv)):
                act.dma_start(bias[:, i, :], b.rearrange("(a n) -> a n", a=1)).then_inc(weights_in, 16)
            for i, b in enumerate((ln1_g, ln1_b, ln2_g, ln2_b, b1)):
                act.dma_start(cols[:, i:i + 1], b.rearrange("(n a) -> n a", a=1)).then_inc(weights_in, 16)
            act.dma_start(wp[:, :, :], Wp.rearrange("(h c) o -> c h o", h=H)).then_inc(weights_in, 16)
            act.dma_start(w1[:, :], W1).then_inc(weights_in, 16)
            act.dma_start(w2[:, :], W2).then_inc(weights_in, 16)
            for i, b in enumerate((bp, b2)):
                act.dma_start(rows[:, i, :], b.rearrange("(a n) -> a n", a=1).broadcast_to([P, C])).then_inc(weights_in, 16)
            act.wait_ge(edges_in, 96)
            act.dma_start(dst_pad[:, 0:PRE], pad_i[:, :]).then_inc(lists_out, 16)
            act.dma_start(dst_pad[:, PADDED - T:PADDED], pad_i[:, 0:T]).then_inc(lists_out, 16)
            act.dma_start(dst_pad[0, PRE:PRE + TILES * T].rearrange("(j p e) -> p j e", p=P, e=T),
                          dst_i.rearrange("p (j e) -> p j e", e=T)).then_inc(lists_out, 16)
            act.wait_ge(ids_f, 1)
            act.dma_start(dst_rows.rearrange("(j p) e -> p j e", p=P),
                          dst_f.rearrange("p (j e) -> p j e", e=T)).then_inc(lists_out, 16)

            def ln_work(s, p):
                cut = slice(p * PT, (p + 1) * PT)
                act.wait_ge(ln_dve, ln_at[s, p])
                if s == 0 and p > 0:
                    act.wait_ge(pool_ln, p)
                if s in (0, 2):
                    nc.scalar.activation(hn[:, cut, :], xs[:, cut, :], ACT.Square).then_inc(ln_act, 1)
                else:
                    st = stat[0:NP, 2 * (s // 2) + 1, cut]
                    nc.scalar.activation(st, st, ACT.Sqrt, bias=eps_col[0:NP, :], scale=1.0 / C).then_inc(ln_act, 1)

            done = 0
            act.wait_ge(ids_pad, 4)
            for i, (s, p) in enumerate(act_order):
                ln_work(s, p)
                if i % 2 == 1 and done < 8:
                    which, q = divmod(done, 4)
                    n = min(4, JB - 4 * q)
                    act.wait_ge(ids_t, done + 1)
                    if done == 4:
                        act.wait_ge(lists_out, 64)
                    to = (src_t, rel_t)[which][:, 4 * q * P:(4 * q + n) * P]
                    nc.scalar.activation(to, banks[done % 4][:, 0:n * P], ACT.Copy).then_inc(ids_c, 1)
                    done += 1
                    if done == 4:
                        act.wait_ge(ids_c, 4)
                        act.dma_start(src_cols, src_t).then_inc(src_out, 16)
            assert done == 8
            act.wait_ge(rel_ok, 1)
            act.dma_start(rel_cols, rel_t).then_inc(lists_out, 16)
            act.wait_ge(lists_out, 80)
            act.wait_ge(src_out, 16)
            act.wait_ge(weights_in, 17 * 16)

        def gpsimd_1(pool):
            nc.gpsimd.memset(src_i[:, TILES - T:TILES], 0).then_inc(ids_pad, 1)
            nc.gpsimd.memset(dst_i[:, TILES - T:TILES], N).then_inc(ids_pad, 1)
            nc.gpsimd.memset(pad_i[:, :], N).then_inc(ids_pad, 1)
            nc.gpsimd.memset(eps_col[:, :], EPS).then_inc(ids_pad, 1)
            nc.gpsimd.memset(ident[:, :], 0.0).then_inc(ident_ok, 1)
            nc.gpsimd.memset(ones[:, :], 1.0).then_inc(ident_ok, 1)
            pool.wait_ge(ident_ok, 2)
            nc.gpsimd.affine_select(out=ident[:, :], in_=ident[:, :], compare_op=ALU.not_equal, fill=1.0,
                                    base=0, pattern=[[-1, P]], channel_multiplier=1).then_inc(ident_ok, 1)
            nc.gpsimd.iota(iota[:, :], [[1, WIDE]], base=0, channel_multiplier=0,
                           allow_small_or_imprecise_dtypes=True).then_inc(ident_ok, 1)
            nc.gpsimd.memset(hnT[0:C, N:NW], 0.0).then_inc(ident_ok, 1)
            pool.wait_ge(ident_ok, 5)
            nc.gpsimd.memset(hnT[C:C + 1, :], 1.0).then_inc(ident_ok, 1)
            pool.wait_ge(ident_ok, 6)
            nc.gpsimd.memset(spread_e[:, :], 0.0).then_inc(ident_ok, 1)
            nc.gpsimd.memset(unit[:, :], 0.0).then_inc(ident_ok, 1)
            pool.wait_ge(ident_ok, 8)

            def final(p):
                cut = slice(p * PT, (p + 1) * PT)
                pool.wait_ge(inv_ok, p + 1)
                nc.gpsimd.tensor_tensor(hn[:, cut, :], xs[:, cut, :],
                                        stat[0:NP, 5, cut].unsqueeze(2).broadcast_to([NP, PT, C]), ALU.mult)\
                  .then_inc(hn_ready, 1)
            for p in range(1, PARTS):
                cut = slice(p * PT, (p + 1) * PT)
                pool.wait_ge(mean_ready, p)
                nc.gpsimd.tensor_tensor(xs[:, cut, :], xs[:, cut, :],
                                        stat[0:NP, 0, cut].unsqueeze(2).broadcast_to([NP, PT, C]), ALU.subtract)\
                  .then_inc(pool_ln, 1)
            for p in range(PARTS - 1):
                final(p)

        def tensor_1(pe):
            pe.wait_ge(ident_ok, 3)
            for which, lst in enumerate((src_f, dst_f)):
                pe.wait_ge(ids_f, 2 - which)
                for q in range(4):
                    n = min(4, JB - 4 * q)
                    if which:
                        pe.wait_ge(ids_c, q + 1)
                    for j in range(4 * q, 4 * q + n):
                        last = nc.tensor.transpose(banks[q][:, (j - 4 * q) * P:(j - 4 * q + 1) * P],
                                                   lst[:, j * P:(j + 1) * P], ident[:, :])
                    last.then_inc(ids_t, 1)
            for q in range(4):
                pe.wait_ge(ids_c, 8)
                nc.tensor.matmul(banks[q][:, 0:TILES // 4], ones[0:1, :], rel_t[0:1, q * (TILES // 4):(q + 1) * (TILES // 4)],
                                 start=True, stop=True).then_inc(base_ps, 1)
            pe.wait_ge(fl_dve, 1)
            nc.tensor.transpose(banks[4][0:1, 0:P], flag[:, 0:1], ident[:, :]).then_inc(fl_pe, 1)
            pe.wait_ge(fl_dve, 2)
            nc.tensor.matmul(banks[4][:, P:P + 1], ones[0:1, :], flag_row[0:1, 1:2], start=True, stop=True).then_inc(fl_pe, 1)

        def vector_1(dve):
            chain = [0]

            def link(ins):
                chain[0] += 1
                ins.then_inc(dve_a, 1)
                dve.wait_ge(dve_a, chain[0])

            dve.wait_ge(edges_in, 96)
            nc.vector.tensor_copy(dst_f, dst_i).then_inc(ids_f, 1)
            nc.vector.tensor_copy(src_f, src_i).then_inc(ids_f, 1)

            def centre(frm, st, cut):
                link(nc.vector.tensor_reduce(st, frm[:, cut, :], X_AXIS, ALU.add))
                link(nc.vector.tensor_scalar(st, st, 1.0 / C, None, ALU.mult))
                nc.vector.tensor_tensor(xs[:, cut, :], frm[:, cut, :], st.unsqueeze(2).broadcast_to([NP, PT, C]),
                                        ALU.subtract).then_inc(ln_dve, 1)

            def segment(s, p):
                cut = slice(p * PT, (p + 1) * PT)
                if s == 0:
                    dve.wait_ge(x_in[p], 32)
                    if p == 0:
                        centre(xs, stat[0:NP, 0, cut], cut)
                    else:
                        link(nc.vector.tensor_reduce(stat[0:NP, 0, cut], xs[:, cut, :], X_AXIS, ALU.add))
                        nc.vector.tensor_scalar(stat[0:NP, 0, cut], stat[0:NP, 0, cut], 1.0 / C, None, ALU.mult)\
                          .then_inc(mean_ready, 1)
                        dve.wait_ge(mean_ready, p)
                        nc.vector.memset(spare[:, :], 0.0).then_inc(ln_dve, 1)
                elif s in (1, 3):
                    dve.wait_ge(ln_act, ln_at[s - 1, p])
                    nc.vector.tensor_reduce(stat[0:NP, s, cut], hn[:, cut, :], X_AXIS, ALU.add)\
                      .then_inc(ln_dve, 1)
                elif s == 2:
                    dve.wait_ge(ln_act, ln_at[1, p])
                    inv = stat[0:NP, 4, cut]
                    link(nc.vector.reciprocal(inv, stat[0:NP, 1, cut]))
                    nc.vector.scalar_tensor_tensor(hs[:, cut, :], xs[:, cut, :], 0.0,
                                                   inv.unsqueeze(2).broadcast_to([NP, PT, C]),
                                                   ALU.max, ALU.mult).then_inc(h_ready, 1)
                    dve.wait_ge(h_ready, p + 1)
                    centre(hs, stat[0:NP, 2, cut], cut)
                else:
                    dve.wait_ge(ln_act, ln_at[3, p])
                    inv = stat[0:NP, 5, cut]
                    if p < PARTS - 1:
                        nc.vector.reciprocal(inv, stat[0:NP, 3, cut]).then_inc(inv_ok, 1)
                    else:
                        link(nc.vector.reciprocal(inv, stat[0:NP, 3, cut]))
                        nc.vector.tensor_tensor(hn[:, cut, :], xs[:, cut, :], inv.unsqueeze(2).broadcast_to([NP, PT, C]),
                                                ALU.mult).then_inc(hn_last, 1)

            for s, p in order:
                segment(s, p)
            dve.wait_ge(ids_t, 4)
            B = TILES // 4
            for q in range(4):
                dve.wait_ge(base_ps, q + 1)
                v = rel_t[:, q * B:(q + 1) * B]
                pair = banks[q][:, 0:B].rearrange("p (m two) -> p m two", two=2)[:, :, 0:1].broadcast_to([P, B // 2, 2])
                link(nc.vector.tensor_tensor(rel_p[:, q * B:(q + 1) * B].rearrange("p (m two) -> p m two", two=2),
                                             v.rearrange("p (m two) -> p m two", two=2), pair, ALU.subtract))
            for q in range(4):
                v = rel_t[:, q * B:(q + 1) * B]
                link(nc.vector.tensor_tensor(v, v, banks[q][:, 0:B], ALU.subtract))
            nc.vector.tensor_reduce(flag[:, 0:1], rel_p, X_AXIS, ALU.max).then_inc(fl_dve, 1)
            dve.wait_ge(fl_pe, 1)
            link(nc.vector.tensor_reduce(flag_row[0:1, 0:1], banks[4][0:1, 0:P], X_AXIS, ALU.max))
            nc.vector.tensor_scalar(flag_row[0:1, 1:2], flag_row[0:1, 0:1], float(NARROW - 1), None, ALU.is_le)\
              .then_inc(fl_dve, 1)
            dve.wait_ge(fl_dve, 2)
            link(nc.vector.tensor_copy(narrow_i[:, :], flag_row[0:1, 1:2]))
            dve.wait_ge(fl_pe, 2)
            link(nc.vector.tensor_copy(flag[:, 1:2], banks[4][:, P:P + 1]))
            link(nc.vector.tensor_tensor(rel_p, rel_p, rel_t, ALU.subtract))
            nc.vector.scalar_tensor_tensor(rel_t, rel_p, flag[:, 1:2], rel_t, ALU.mult, ALU.add).then_inc(rel_ok, 1)
            dve.wait_ge(rel_ok, 1)

        gathered = [sem(f"gathered{i}") for i in range(2 * NG)]
        attrs_in = [sem(f"attrs_in{i}") for i in range(2 * NG)]
        meta_in = [sem(f"meta_in{i}") for i in range(2)]
        z_ones = sem("z_ones")
        hn_t = sem("hn_t")
        hn_c = sem("hn_c")
        acc_zero = sem("acc_zero")
        w_dve = sem("w_dve")
        w_pe = sem("w_pe")
        w_act = sem("w_act")
        uw_ready, uw_sb = sem("uw_ready"), sem("uw_sb")
        zt_ready, zt_sb = sem("zt_ready"), sem("zt_sb")
        sc_ready, sc_read, alpha_ready = sem("sc_ready"), sem("sc_read"), sem("alpha_ready")
        wmat_ready, tiles_summed, acc_added = sem("wmat_ready"), sem("tiles_summed"), sem("acc_added")
        alphaT_ready, top_ready, ends_ready = sem("alphaT_ready"), sem("top_ready"), sem("ends_ready")
        ends_top, ends_cols = sem("ends_top"), sem("ends_cols")
        fade_ready, fade_ps, logw_ready, logwT, wexp_ready = (sem("fade_ready"), sem("fade_ps"), sem("logw_ready"),
                                                              sem("logwT"), sem("wexp_ready"))
        drop_ready = sem("drop_ready")
        dve_b = sem("dve_b")
        scan_done = sem("scan_done")

        passed = {nc.tensor: sem("pe_passed"), nc.gpsimd: sem("pool_passed")}

        def wait_apart(eng, signal, value):
            eng.wait_ge(signal, value)
            eng.sem_inc(passed[eng if eng in passed else (nc.tensor if eng.engine == ENG.PE else nc.gpsimd)], 1)

        def slot(par, g):
            return par * NG + g

        def over_chunks(eng, first, body, last):
            c = first
            if c % 2:
                body(c, 1, c // 2)
                c += 1
            pairs = (last - c) // 2
            with eng.Fori(c // 2, c // 2 + pairs) as i:
                body(i * 2, 0, i)
                body(i * 2 + 1, 1, i)
            if c + 2 * pairs < last:
                body(last - 1, (last - 1) % 2, (last - 1) // 2)

        def edge_phase(W, TB, span=None):
            BT = 256 // W
            NB = K // BT
            PB = BT // TB
            ZB = min(4, BT)
            HB = BT // ZB
            UN = H * (span or PB * W)

            def windows(eng, keys_ap, b, n=PB):
                first = 1 + 2 * b * BT
                _, v = nc.values_load_multi_w_load_instructions(
                    keys_ap[0:1, first:first + 2 * TB * (n - 1) + 1:2 * TB], engines=(eng,), min_val=0, max_val=N,
                    skip_runtime_bounds_check_because="dst is a node or the padding's node N")
                return v

            def offset(v, w):
                return nc.s_assert_within(v[w] - v[0], 0, span - W,
                                          skip_runtime_bounds_check_because="every pair of tiles fits a window on this path")

            def pe_scores(pe, c, par, half, b, v):
                if not (isinstance(c, int) and c == 0 and b == 0):
                    pe.wait_ge(uw_sb, c * NB + b)
                width = span or W
                for w, first in enumerate(v):
                    for h in range(H):
                        last = nc.tensor.matmul(uw_ps[0:Z, (w * H + h) * width:(w * H + h + 1) * width], amat[:, h, :],
                                                hnT[:, bass.ds(first, width)], start=True, stop=True)
                last.then_inc(uw_ready, 1)
                if b * BT % G == 0:
                    g = b * BT // G
                    pe.wait_ge(gathered[slot(par, g)], half * (16 * G) + 16 * G)
                    extra = 16 if isinstance(c, int) and c == CHUNKS - 1 and g == NG - 1 else 0
                    pe.wait_ge(attrs_in[slot(par, g)], half * 16 + 16 + extra)
                for j in range(HB):
                    bank = (b * HB + j) % 2
                    if not (isinstance(c, int) and c == 0 and b * HB + j < 2):
                        pe.wait_ge(zt_sb, c * (NB * HB) + (b * HB + j - 1))
                    for i in range(ZB):
                        k = par * K + b * BT + j * ZB + i
                        last = nc.tensor.transpose(zt_ps[bank][0:Z, i * T:(i + 1) * T], z[:, k, :], ident[:, :])
                    last.then_inc(zt_ready, 1)

            def pe_scores_end(pe, c, par, half, b):
                cut = [uwin[:, w * H * W:(w + 1) * H * W] for w in range(PB)]
                if span:
                    v = windows(ENG.PE, keys[:, par, :], b)
                    cut = [uwin[:, 0:H * span].rearrange("z (h n) -> z h n", h=H)
                           [:, :, bass.ds(offset(v, w) if w else 0, W)]
                           for w in range(PB)]
                pe.wait_ge(uw_sb, c * NB + (b + 1))
                if not (isinstance(c, int) and c == 0 and b < 2):
                    pe.wait_ge(sc_read, c * NB + (b - 1))
                for j in range(HB):
                    pe.wait_ge(zt_sb, c * (NB * HB) + (b * HB + j + 1))
                    for i in range(ZB):
                        t = j * ZB + i
                        w = t // TB
                        last = nc.tensor.matmul(sc_ps[b % 2][:, t * H * W:(t + 1) * H * W],
                                                zT[:, b % 2, t * T:(t + 1) * T],
                                                cut[w], start=True, stop=True)
                last.then_inc(sc_ready, 1)

            def pe_sums(pe, c, par, b):
                pe.wait_ge(wmat_ready, c * NB + (b + 1))
                if not (isinstance(c, int) and c == 0 and b < 2):
                    pe.wait_ge(acc_added, c * (NB * PB) + (b - 1) * PB)
                for t in range(BT):
                    w = t // TB
                    last = nc.tensor.matmul(ag_ps[b % 2][0:Z, w * H * W:(w + 1) * H * W], z[:, par * K + b * BT + t, :],
                                            wmat[:, b % 2, t * H * W:(t + 1) * H * W],
                                            start=(t % TB == 0), stop=(t % TB == TB - 1))
                last.then_inc(tiles_summed, BT)

            def pe_scan(pe, c):
                wait_apart(pe, alpha_ready, c * NB + NB)
                if not (isinstance(c, int) and c == 0):
                    wait_apart(pe, wexp_ready, c)
                nc.tensor.transpose(sn_ps[0:R, 0:T], alpha[:, :, :].rearrange("p h k -> p (h k)"), ident[:, :])\
                  .then_inc(alphaT_ready, 1)
                wait_apart(pe, top_ready, c + 1)
                ends = sn_ps[0:1, T:2 * T].rearrange("a (r two) -> a r two", two=2)
                nc.tensor.transpose(ends[:, :, 0], top[:, 0:1], ident[0:R, 0:R])
                nc.tensor.transpose(ends[:, :, 1], top[:, T - 1:T], ident[0:R, 0:R]).then_inc(ends_ready, 1)
                wait_apart(pe, ends_top, c * H + H)
                rows_v = top_ends[:, :, :].rearrange("a h (k two) -> a (h k) two", two=2)
                for j in range(2):
                    last = nc.tensor.matmul(sn_ps[0:R, 2 * T + j:2 * T + j + 1], rows_v[:, :, j], ones[0:1, 0:1],
                                            start=True, stop=True)
                last.then_inc(ends_cols, 1)
                pe.wait_ge(fade_ready, c + 1)
                nc.tensor.matmul(sn_ps[0:Z, 2 * T + 2:2 * T + 4], ones[0:1, 0:Z], fade[0:1, :], start=True, stop=True)\
                  .then_inc(fade_ps, 1)
                wait_apart(pe, logw_ready, c + 1)
                nc.tensor.transpose(sn_ps[:, 2 * T + R:2 * T + 2 * R], top2[:, :], ident[0:R, 0:R]).then_inc(logwT, 1)

            def pe_step(pe, c, par, half, sums=True):
                wait_apart(pe, meta_in[par], half * 64 + 64)
                v = windows(ENG.PE, keys[:, par, :], 0, 1 if span else PB)
                for b in range(NB):
                    pe_scores(pe, c, par, half, b, v)
                    if sums:
                        pe_sums(pe, c - 1, 1 - par, b)
                    if b + 1 < NB:
                        v = windows(ENG.PE, keys[:, par, :], b + 1, 1 if span else PB)
                    pe_scores_end(pe, c, par, half, b)
                pe_scan(pe, c)

            def tensor(pe):
                pe_step(pe, 0, 0, 0, sums=False)
                over_chunks(pe, 1, lambda c, par, half: pe_step(pe, c, par, half), CHUNKS - 1)
                pe_step(pe, CHUNKS - 1, 1, CHUNKS // 2 - 1)
                for b in range(NB):
                    pe_sums(pe, CHUNKS - 1, 1, b)

            def act_step(act, c, par, half):
                for b in range(NB):
                    act.wait_ge(uw_ready, c * NB + (b + 1))
                    if not (isinstance(c, int) and c == 0 and b == 0):
                        act.wait_ge(sc_ready, c * NB + b)
                    nc.scalar.activation(uwin[:, 0:UN], uw_ps[0:Z, 0:UN], ACT.Copy).then_inc(uw_sb, 1)
                    for j in range(HB):
                        act.wait_ge(zt_ready, c * (NB * HB) + (b * HB + j + 1))
                        nc.scalar.activation(zT[:, b % 2, j * ZB * T:(j + 1) * ZB * T], zt_ps[(b * HB + j) % 2][0:Z, 0:ZB * T],
                                             ACT.Copy).then_inc(zt_sb, 1)
                act.wait_ge(drop_ready, c + 1)
                nc.scalar.activation(fade[:, :], drop[:, :], ACT.Exp).then_inc(fade_ready, 1)
                act.wait_ge(logwT, c + 1)
                if not (isinstance(c, int) and c == 0):
                    act.wait_ge(wmat_ready, c * NB)
                nc.scalar.activation(wexp[:, :, :].rearrange("p h k -> p (h k)"), sn_ps[:, 2 * T + R:2 * T + 2 * R],
                                     ACT.Exp).then_inc(wexp_ready, 1)

            def scalar(act):
                act_step(act, 0, 0, 0)
                over_chunks(act, 1, lambda c, par, half: act_step(act, c, par, half), CHUNKS)

            IN_SUMS, IN_SCORES, IN_SCAN = NB, NB, 14
            per_step = IN_SUMS + IN_SCORES + IN_SCAN

            class Own:
                def __init__(self, dve, start):
                    self.dve, self.start, self.n = dve, start, 0

                def link(self, ins):
                    self.n += 1
                    ins.then_inc(dve_b, 1)
                    self.dve.wait_ge(dve_b, self.start + self.n)

            def dve_pick(own, offsets, b):
                own.link(nc.vector.tensor_tensor(
                    pick[:, :].rearrange("p (t w) -> p t w", w=W),
                    iota[:, 0:W].unsqueeze(1).broadcast_to([P, BT, W]),
                    offsets[:, b * BT:(b + 1) * BT].unsqueeze(2).broadcast_to([P, BT, W]), ALU.is_equal))

            def picked():
                return pick[:, :].rearrange("p (t w) -> p t w", w=W).unsqueeze(2).broadcast_to([P, BT, H, W])

            def four(ap):
                return ap.rearrange("p (t h w) -> p t h w", h=H, w=W)

            def dve_weights(dve, own, c, b):
                dve_pick(own, rel_b[:, :], b)
                if b == 0:
                    dve.wait_ge(wexp_ready, c + 1)
                if not (isinstance(c, int) and c == 0 and b < 2):
                    dve.wait_ge(tiles_summed, c * K + (b - 1) * BT)
                w = wexp[:, :, b * BT:(b + 1) * BT].rearrange("p h t -> p t h").unsqueeze(3).broadcast_to([P, BT, H, W])
                nc.vector.tensor_tensor(four(wmat[:, b % 2, :]), picked(), w, ALU.mult).then_inc(wmat_ready, 1)
                dve.wait_ge(wmat_ready, c * NB + (b + 1))

            def dve_add(dve, c, b, v):
                dve.wait_ge(tiles_summed, c * K + (b + 1) * BT)
                for w in range(PB):
                    if not (isinstance(c, int) and c == 0 and b + w == 0):
                        dve.wait_ge(acc_added, c * (NB * PB) + (b * PB + w))
                    a = acc[0:Z, :, bass.ds(v[w], W)]
                    nc.vector.tensor_tensor(a, a, ag_ps[b % 2][0:Z, w * H * W:(w + 1) * H * W]
                                            .rearrange("p (h w) -> p h w", h=H), ALU.add).then_inc(acc_added, 1)

            def dve_scores(dve, own, c, par, half, b):
                if b == 0:
                    dve.wait_ge(meta_in[par], half * 64 + 64)
                dve_pick(own, rel[:, par, :], b)
                dve.wait_ge(sc_ready, c * NB + (b + 1))
                if not (isinstance(c, int) and c == 0 and b == 0):
                    dve.wait_ge(alpha_ready, c * NB + b)
                nc.vector.tensor_tensor(four(prod[:, :]), four(sc_ps[b % 2][:, :]), picked(), ALU.mult).then_inc(sc_read, 1)
                dve.wait_ge(sc_read, c * NB + (b + 1))
                if b == 0 and not (isinstance(c, int) and c == 0):
                    dve.wait_ge(alphaT_ready, c)
                nc.vector.tensor_reduce(alpha[:, :, b * BT:(b + 1) * BT].rearrange("p h t -> p t h"),
                                        four(prod[:, :]), X_AXIS, ALU.add).then_inc(alpha_ready, 1)

            def dve_scan(dve, own, c, par):
                d = drow[:, par, :]
                kk = keys[:, par, :]
                _, open_node = nc.values_load_multi_w_load_instructions(
                    kk[0:1, 0:1], engines=(ENG.DVE,), min_val=0, max_val=N,
                    skip_runtime_bounds_check_because="dst is a node or the padding's node N")
                own.link(nc.vector.tensor_tensor(keep[:, 1:T], d[:, 1:T], d[:, 0:T - 1], ALU.is_equal))
                own.link(nc.vector.tensor_scalar(keep[:, 1:T], keep[:, 1:T], 2 * BIG, -BIG, ALU.mult, ALU.add))
                own.link(nc.vector.tensor_tensor(keep2[:, 0:2 * K], kk[:, 1:2 * K + 1], kk[:, 0:2 * K], ALU.is_equal))
                own.link(nc.vector.tensor_scalar(keep2[:, 0:2 * K], keep2[:, 0:2 * K], 2 * BIG, -BIG, ALU.mult, ALU.add))
                dve.wait_ge(alphaT_ready, c + 1)
                own.link(nc.vector.tensor_tensor_scan(far[:, :], keep[:, 0:T], sn_ps[0:R, 0:T], -BIG, ALU.min, ALU.max))
                nc.vector.tensor_tensor_scan(top[:, T - 1::-1], keep[:, T:0:-1], far[:, T - 1::-1], -BIG, ALU.min, ALU.max)\
                  .then_inc(top_ready, 1)
                dve.wait_ge(ends_ready, c + 1)
                for h in range(H):
                    ins = nc.vector.tensor_tensor_scan(fwd2[:, h, :], keep2[:, 0:2 * K], sn_ps[0:1, T + h * 2 * K:T + (h + 1) * 2 * K],
                                                       carry[:, h:h + 1], ALU.min, ALU.max)
                    own.link(ins)
                for h in range(H):
                    nc.vector.tensor_tensor_scan(top_ends[:, h, ::-1], keep2[:, 2 * K:0:-1], fwd2[:, h, ::-1], -BIG,
                                                 ALU.min, ALU.max).then_inc(ends_top, 1)
                dve.wait_ge(ends_top, c * H + H)
                own.link(nc.vector.scalar_tensor_tensor(gone[:, :], top_ends[:, :, 0], keep2[0:1, 0:1], carry[:, :], ALU.min, ALU.max))
                nc.vector.tensor_tensor(drop[:, :], carry[:, :], gone[:, :], ALU.subtract).then_inc(drop_ready, 1)
                dve.wait_ge(drop_ready, c + 1)
                own.link(nc.vector.tensor_copy(carry[:, :], top_ends[:, :, 2 * K - 1]))
                own.link(nc.vector.tensor_scalar(far[:, :], d, d[:, 0:1], -BIG, ALU.not_equal, ALU.mult))
                dve.wait_ge(ends_cols, c + 1)
                dve.wait_ge(fade_ps, c + 1)
                own.link(nc.vector.scalar_tensor_tensor(top2[:, :], far[:, :], sn_ps[0:R, 2 * T:2 * T + 1], top[:, :], ALU.add, ALU.max))
                own.link(nc.vector.tensor_scalar(far[:, :], d, d[:, T - 1:T], -BIG, ALU.not_equal, ALU.mult))
                own.link(nc.vector.scalar_tensor_tensor(top[:, :], far[:, :], sn_ps[0:R, 2 * T + 1:2 * T + 2], top2[:, :], ALU.add, ALU.max))
                if isinstance(c, int) and c == 0:
                    dve.wait_ge(acc_zero, 3)
                else:
                    dve.wait_ge(acc_added, c * (NB * PB))
                node = acc[0:Z, :, bass.ds(open_node[0], 1)]
                own.link(nc.vector.tensor_tensor(node, node, sn_ps[0:Z, 2 * T + 2:2 * T + 4].unsqueeze(2), ALU.mult))
                nc.vector.tensor_tensor(top2[:, :], sn_ps[0:R, 0:T], top[:, :], ALU.subtract).then_inc(logw_ready, 1)
                nc.vector.tensor_copy(rel_b[:, :], rel[:, par, :])
                nc.vector.tensor_copy(keys_b[:, :], kk).then_inc(scan_done, 1)
                dve.wait_ge(scan_done, c + 1)

            def dve_step(dve, c, par, half, sums=True):
                start = (c - 1) * per_step + (IN_SCORES + IN_SCAN) if sums else 0
                own = Own(dve, start)
                if sums:
                    dve_weights(dve, own, c - 1, 0)
                for b in range(NB):
                    if sums and b + 1 < NB:
                        dve_weights(dve, own, c - 1, b + 1)
                    if sums:
                        dve.wait_ge(scan_done, c)
                        nc.vector.memset(spare[:, :], 0.0)
                        v = windows(ENG.DVE, keys_b[:, :], b)
                    dve_scores(dve, own, c, par, half, b)
                    if sums:
                        dve_add(dve, c - 1, b, v)
                dve_scan(dve, own, c, par)
                assert own.n == (per_step if sums else IN_SCORES + IN_SCAN), own.n

            def vector(dve):
                dve_step(dve, 0, 0, 0, sums=False)
                over_chunks(dve, 1, lambda c, par, half: dve_step(dve, c, par, half), CHUNKS)
                own = Own(dve, (CHUNKS - 1) * per_step + IN_SCORES + IN_SCAN)
                dve_weights(dve, own, CHUNKS - 1, 0)
                for b in range(NB):
                    if b + 1 < NB:
                        dve_weights(dve, own, CHUNKS - 1, b + 1)
                    nc.vector.memset(spare[:, :], 0.0)
                    dve_add(dve, CHUNKS - 1, b, windows(ENG.DVE, keys_b[:, :], b))
                dve.wait_ge(acc_added, CHUNKS * NB * PB)

            return tensor, scalar, vector

        narrow_phase = edge_phase(NARROW, 2, SPAN)
        wide_phase = edge_phase(WIDE, 1)

        def either(engine, builder, which):
            _, v = nc.values_load_multi_w_load_instructions(narrow_i[0:1, 0:1], engines=(engine,), min_val=0, max_val=1,
                                                            skip_runtime_bounds_check_because="a comparison's result")
            with builder.If(v[0] > 0):
                narrow_phase[which](builder)
            with builder.Else():
                wide_phase[which](builder)

        with nc.Block() as block:
            def join(eng, waits=True):
                eng.sem_inc(stage1_done, 1)
                if waits:
                    eng.wait_ge(stage1_done, 5)

            @block.gpsimd
            def _(pool):
                gpsimd_1(pool)
                join(pool, waits=False)
                pool.wait_ge(table_out, PARTS * 64)
                pool.wait_ge(ids_t, 8)
                pool.wait_ge(lists_out, 64)

                def gather(c, par, half):
                    for g in range(NG):
                        if g == 0:
                            wait_apart(pool, idx_in[par], half * 16 + 16)
                        if not (isinstance(c, int) and c < 2):
                            wait_apart(pool, tiles_summed, (c - 2) * K + (g + 1) * G)
                        for k in range(g * G, (g + 1) * G):
                            pool.indirect_dma_start(z[:, par * K + k, 0:C], None, table,
                                                    bass.IndirectOffsetOnAxis(ap=idx[:, par, k:k + 1], axis=0))\
                                .then_inc(gathered[slot(par, g)], 16)
                gather(0, 0, 0)
                gather(1, 1, 0)
                over_chunks(pool, 2, gather, CHUNKS)

            @block.sync
            def _(sp):
                sync_1(sp)
                join(sp)

                def attrs(c, par, g):
                    cols_ = z[:, par * K + g * G:par * K + (g + 1) * G, C:C + CE]
                    first = (c * NG + g) * G * T
                    sp.dma_start(cols_, edge_attr[bass.ds(first, G * T), :].rearrange("(k p) f -> p k f", p=T))\
                      .then_inc(attrs_in[slot(par, g)], 16)

                def loads(c, par, half, last=False):
                    early = isinstance(c, int) and c < 2
                    if not early:
                        for g in range(NG):
                            sp.wait_ge(gathered[slot(par, g)], half * (16 * G))
                        sp.dma_start(idx[:, par, :], src_cols[:, bass.ds(c * K, K)]).then_inc(idx_in[par], 16)
                    if not early:
                        sp.wait_ge(scan_done, c - 1)
                    sp.dma_start(rel[:, par, :], rel_cols[:, bass.ds(c * K, K)]).then_inc(meta_in[par], 16)
                    ends = dst_pad[0, bass.ds(c * (K * T) + (PRE - 1), (K + 1) * T)].rearrange("(k e) -> k e", e=T)[:, 0:2]
                    sp.dma_start(keys[:, par, :].rearrange("a (k two) -> a k two", two=2), ends.unsqueeze(0))\
                      .then_inc(meta_in[par], 16)
                    for h in range(H):
                        sp.dma_start(drow[h * K:(h + 1) * K, par, :], dst_rows[bass.ds(c * K, K), :]).then_inc(meta_in[par], 16)
                    for g in range(NG):
                        if not early:
                            sp.wait_ge(tiles_summed, (c - 2) * K + (g + 1) * G)
                        if last and g == NG - 1:
                            k0, e0 = par * K + g * G, (TILES - G) * T
                            sp.dma_start(z[:, k0:k0 + LAST_TILES, C:C + CE],
                                         edge_attr[e0:e0 + LAST_TILES * T, :].rearrange("(k p) f -> p k f", p=T))\
                              .then_inc(attrs_in[slot(par, g)], 16)
                            sp.dma_start(z[0:LAST_ROWS, k0 + LAST_TILES, C:C + CE], edge_attr[e0 + LAST_TILES * T:E, :])\
                              .then_inc(attrs_in[slot(par, g)], 16)
                        else:
                            attrs(c, par, g)
                loads(0, 0, 0)
                loads(1, 1, 0)
                over_chunks(sp, 2, lambda c, par, half: loads(c, par, half), CHUNKS - 2)
                loads(CHUNKS - 2, 0, CHUNKS // 2 - 1)
                loads(CHUNKS - 1, 1, CHUNKS // 2 - 1, last=True)

            @block.tensor
            def _(pe):
                tensor_1(pe)
                join(pe)
                for q in range(NT // OT):
                    if q >= 4:
                        pe.wait_ge(hn_c, q - 3)
                    for t in range(OT):
                        last = nc.tensor.transpose(hn_ps[q % 4][0:C, t * NP:(t + 1) * NP], hn[:, q * OT + t, :], ident[0:NP, 0:NP])
                    last.then_inc(hn_t, 1)
                pe.wait_ge(w_dve, 1)
                uz, uh = unit[:, 0:Z], unit[:, Z:Z + C + 1]
                for i, (w, last_row) in enumerate(((wq, 0), (wk, 1), (wv, 2))):
                    n = C + 1 if i == 0 else Z
                    for h in range(H):
                        o = banks[3 + i][0:C, h * 128:h * 128 + n]
                        hc = slice(h * C, (h + 1) * C)
                        nc.tensor.matmul(o, w[:, hc], spread_q[:, :] if i == 0 else spread[:, :], start=True, stop=False)
                        if i:
                            nc.tensor.matmul(o, we[:, hc], spread_e[:, :], start=False, stop=False)
                        last = nc.tensor.matmul(o, bias[:, i, hc], uh if i == 0 else uz, start=False, stop=True)
                    last.then_inc(w_pe, 1)
                pe.wait_ge(w_act, 3)
                for h in range(H):
                    last = nc.tensor.matmul(banks[6][0:C + 1, h * 128:h * 128 + Z], wqT[:, h, :], wkT[:, h, :], start=True, stop=True)
                last.then_inc(w_pe, 1)
                for h in range(H):
                    last = nc.tensor.matmul(banks[7][0:Z, h * 128:h * 128 + C], wvT[:, h, :], wp[:, h, :], start=True, stop=True)
                last.then_inc(w_pe, 1)
                nc.tensor.matmul(banks[2][0:C, 0:1], w1[:, :], cols[:, 3:4], start=True, stop=True).then_inc(w_pe, 1)
                pe.wait_ge(w_act, 5)
                pe.wait_ge(hn_c, NT // OT)
                pe.wait_ge(w_dve, 2)
                pe.wait_ge(z_ones, 1)
                either(ENG.PE, pe, 0)

            @block.scalar
            def _(act):
                scalar_1(act)
                join(act)

                def columns(q):
                    act.wait_ge(hn_t, q + 1)
                    v = hnT[0:C, 0:N].rearrange("c (p t) -> c t p", t=NT)[:, q * OT:(q + 1) * OT, :]
                    nc.scalar.activation(v, hn_ps[q % 4][0:C, 0:OT * NP].rearrange("c (t p) -> c t p", p=NP), ACT.Copy)\
                      .then_inc(hn_c, 1)
                for q in range(NT // OT):
                    columns(q)
                for i, (w, n) in enumerate(((wqT, C + 1), (wkT, Z), (wvT, Z))):
                    act.wait_ge(w_pe, i + 1)
                    nc.scalar.activation(w[:, :, :], banks[3 + i][0:C, 0:256].rearrange("c (h n) -> c h n", h=H)[:, :, 0:n],
                                         ACT.Copy).then_inc(w_act, 1)
                act.wait_ge(w_pe, 4)
                nc.scalar.activation(amat[:, :, :], banks[6][0:C + 1, 0:256].rearrange("c (h n) -> c h n", h=H)[:, :, 0:Z],
                                     ACT.Copy, scale=1.0 / np.sqrt(C).item()).then_inc(w_act, 1)
                act.wait_ge(w_pe, 5)
                nc.scalar.activation(vmat[:, :, 0:C], banks[7][0:Z, 0:256].rearrange("c (h n) -> c h n", h=H)[:, :, 0:C],
                                     ACT.Copy).then_inc(w_act, 1)
                either(ENG.Activation, act, 1)

            @block.vector
            def _(dve):
                vector_1(dve)
                join(dve)
                k = [0]

                def link(ins):
                    k[0] += 1
                    ins.then_inc(w_late, 1)
                    dve.wait_ge(w_late, k[0])
                nc.vector.memset(z[:, :, Z - 1:Z], 1.0).then_inc(z_ones, 1)
                hn_at, hn_to = NT * C, 2 * NT * C
                link(nc.vector.memset(spread[:, :], 0.0))
                g, b = cols[:, 0:1], cols[:, 1:2]
                link(nc.vector.tensor_scalar(spread[:, 0:C], ident[0:C, 0:C], g, None, ALU.mult))
                link(nc.vector.tensor_copy(spread[:, Z - 1:Z], b))
                link(nc.vector.tensor_scalar(spread_q[:, 0:C], ident[0:C, 0:C], g, None, ALU.mult))
                link(nc.vector.tensor_copy(spread_q[:, C:C + 1], b))
                link(nc.vector.tensor_copy(spread_e[:, C:C + CE], ident[0:CE, 0:CE]))
                link(nc.vector.memset(unit[:, Z - 1:Z], 1.0))
                nc.vector.memset(unit[:, Z + C:Z + C + 1], 1.0).then_inc(w_dve, 1)
                link(nc.vector.memset(keep[:, :], -BIG))
                link(nc.vector.memset(keep2[:, :], -BIG))
                link(nc.vector.memset(carry[:, :], 0.0))
                link(nc.vector.tensor_copy(vmat[:, :, C:C + 1].rearrange("z h a -> z (h a)"),
                                           ident[0:Z, Z - 1:Z].broadcast_to([Z, H])))
                nc.vector.memset(arena[0:Z, 0:hn_at], 0.0).then_inc(acc_zero, 1)
                nc.vector.memset(arena[0:Z, hn_to:H * NW], 0.0).then_inc(acc_zero, 1)
                dve.wait_ge(w_pe, 6)
                link(nc.vector.tensor_tensor(b1c[:, :], banks[2][0:C, 0:1], cols[:, 4:5], ALU.add))
                nc.vector.tensor_scalar(w1[:, :], w1[:, :], cols[:, 2:3], None, ALU.mult).then_inc(w_dve, 1)
                dve.wait_ge(w_dve, 2)
                dve.wait_ge(hn_c, NT // OT)
                nc.vector.memset(arena[0:Z, hn_at:hn_to], 0.0).then_inc(acc_zero, 1)
                either(ENG.DVE, dve, 2)

        at = [0]

        def room(n, shape_to, np_=NP):
            v = zflat[0:np_, at[0]:at[0] + n]
            at[0] += n
            return v.rearrange(*shape_to[0:1], **shape_to[1])

        tc_ = ("p (t c) -> p t c", dict(c=C))
        GS = OT * C
        st = [room(H * OT * NP, ("z (h t p) -> z h t p", dict(h=H, t=OT)), Z) for _ in range(2)]
        hb = [room(GS, tc_) for _ in range(2)]
        xb = [room(GS, tc_) for _ in range(2)]
        oo = [room(GS, tc_) for _ in range(2)]
        on = [room(GS, tc_) for _ in range(2)]
        assert at[0] <= 2 * K * Z
        oc = node_room[0:NP, 0:NT * C].rearrange("p (t c) -> p t c", c=C)
        ob = node_room[0:NP, NT * C:2 * NT * C].rearrange("p (t c) -> p t c", c=C)
        o1 = [prod[0:NP, i * GS:(i + 1) * GS].rearrange("p (t c) -> p t c", c=C) for i in range(2)]
        osq = [wmat[0:NP, 0, i * GS:(i + 1) * GS].rearrange("p (t c) -> p t c", c=C) for i in range(2)]
        fin = [wmat[0:NP, 1, i * GS:(i + 1) * GS].rearrange("p (t c) -> p t c", c=C) for i in range(2)]
        oT = [zT[0:C, 0, i * 512:i * 512 + OT * NP] for i in range(2)]
        hT = [zT[0:C, 1, i * 512:i * 512 + OT * NP] for i in range(2)]
        den = [stat[0:NP, 0:H, i * OT:(i + 1) * OT] for i in range(2)]
        den_r = [stat[0:NP, 2:2 + H, i * OT:(i + 1) * OT] for i in range(2)]
        mean = [stat[0:NP, 4, i * OT:(i + 1) * OT] for i in range(2)]
        var = stat[0:NP, 5, :]

        def of(v, g, n=1):
            return v[:, bass.ds(g * OT, n * OT)]

        hx_in = [sem(f"hx_in{i}") for i in range(2)]
        out_done = [sem(f"out_done{i}") for i in range(2)]
        st_ready, pr_ready, pr_read = sem("st_ready"), sem("pr_ready"), sem("pr_read")
        hbp_ready, xb_ready, o_ready, ox_ready = sem("hbp_ready"), sem("xb_ready"), sem("o_ready"), sem("ox_ready")
        oc_ready, sq_ready, var_ready, sd_ready, norm_ready = (sem("oc_ready"), sem("sq_ready"), sem("var_ready"),
                                                               sem("sd_ready"), sem("norm_ready"))
        oT_ps, oT_sb, hid_ps, hid_sb, y_ps, fin_ready = (sem("oT_ps"), sem("oT_sb"), sem("hid_ps"), sem("hid_sb"),
                                                         sem("y_ps"), sem("fin_ready"))
        dve_c = sem("dve_c")
        inv_ready = sem("inv_ready")
        LINKS = 6

        LAG = 3

        def there(g):
            return not isinstance(g, int) or 0 <= g < OGROUPS

        def slots(eng, slot):
            def one(g):
                b = g - LAG
                slot(g, g % 2, b, b % 2, (b - 1) // 2, g // 2 if g % 2 == 0 and g < OGROUPS else None)
            peeled = LAG + 4
            for g in range(peeled):
                one(g)
            with eng.Fori((peeled - LAG) // 2, OGROUPS // 2 - 2) as i:
                slot(i * 2 + LAG, 1, i * 2, 0, i - 1, None)
                slot(i * 2 + (LAG + 1), 0, i * 2 + 1, 1, i, i + 2)
            for g in range(OGROUPS - 2, OGROUPS + LAG + 1):
                one(g)

        with nc.Block() as block:
            @block.sync
            def _(sp):
                def load(g, s):
                    for v, to in ((h_v, hb[s]), (x_v, xb[s])):
                        node_dma(sp, to, v[:, bass.ds(g * OT, OT), :], hx_in[s])

                def store(g, s):
                    sp.wait_ge(fin_ready, g + 1)
                    node_dma(sp, out_v[:, bass.ds(g * OT, OT), :], fin[s], out_done[s])

                def following(g, s):
                    sp.wait_ge(ox_ready, g - 1)
                    load(g, s)

                BEHIND = LAG + 1
                load(0, 0)
                load(1, 1)
                for g in range(2, BEHIND):
                    following(g, g % 2)
                with sp.Fori(BEHIND // 2, OGROUPS // 2) as i:
                    for s in range(2):
                        following(i * 2 + s, s)
                        store(i * 2 + (s - BEHIND), s)
                following(OGROUPS - 1, 0)
                for g in range(OGROUPS - 1 - BEHIND, OGROUPS):
                    store(g, g % 2)
                sp.wait_ge(out_done[0], (OGROUPS + 1) // 2 * 32)
                sp.wait_ge(out_done[1], OGROUPS // 2 * 32)

            @block.scalar
            def _(act):
                def pack(g, s):
                    if not isinstance(g, int) or g > 1:
                        act.wait_ge(pr_ready, g - 1)
                    v = acc[0:Z, :, 0:N].rearrange("z h (p t) -> z h t p", t=NT)[:, :, bass.ds(g * OT, OT), :]
                    for h in range(H):
                        nc.scalar.activation(st[s][:, h], v[:, h], ACT.Copy).then_inc(st_ready, 1)

                def slot(g, s, b, z, half, e):
                    if there(b):
                        act.wait_ge(oT_ps, b + 1)
                        nc.scalar.activation(oT[z], banks[4][0:C, 0:OT * NP], ACT.Copy).then_inc(oT_sb, 1)
                    if there(g + 1):
                        pack(g + 1, 1 - s)
                    if there(g):
                        act.wait_ge(oc_ready, g + 1)
                        nc.scalar.activation(osq[s], of(oc, g), ACT.Square).then_inc(sq_ready, 1)
                    if e is not None:
                        act.wait_ge(var_ready, g + 1)
                        n = 1 if isinstance(e, int) and e == 0 else 2
                        v = of(var, g - (n - 1), n)
                        nc.scalar.activation(v, v, ACT.Sqrt, bias=eps_col[0:NP, :], scale=1.0 / C).then_inc(sd_ready, 1)
                    if there(b):
                        act.wait_ge(hid_ps, b + 1)
                        nc.scalar.activation(hT[z], banks[5][0:C, 0:OT * NP], ACT.Gelu, bias=b1c[:, :]).then_inc(hid_sb, 1)

                pack(0, 0)
                slots(act, slot)

            @block.gpsimd
            def _(pool):
                def body(g, s, i):
                    pool.wait_ge(hx_in[s], i * 64 + 64)
                    nc.gpsimd.tensor_tensor(hb[s], hb[s], rows[0:NP, 0, :].unsqueeze(1).broadcast_to([NP, OT, C]), ALU.add)\
                      .then_inc(hbp_ready, 1)
                    nc.gpsimd.tensor_tensor(xb[s], xb[s], rows[0:NP, 1, :].unsqueeze(1).broadcast_to([NP, OT, C]), ALU.add)\
                      .then_inc(xb_ready, 1)
                    pool.wait_ge(o_ready, g + 1)
                    pool.wait_ge(xb_ready, g + 1)
                    nc.gpsimd.tensor_tensor(of(ob, g), oo[s], xb[s], ALU.add).then_inc(ox_ready, 1)
                body(0, 0, 0)
                body(1, 1, 0)
                with pool.Fori(1, OGROUPS // 2) as i:
                    body(i * 2, 0, i)
                    body(i * 2 + 1, 1, i)
                body(OGROUPS - 1, 0, OGROUPS // 2)

            @block.tensor
            def _(pe):
                def project(g, s):
                    pe.wait_ge(st_ready, g * H + H)
                    if not (isinstance(g, int) and g < 2):
                        pe.wait_ge(pr_read, g * H - H)
                    for h in range(H):
                        for t in range(OT):
                            last = nc.tensor.matmul(banks[2 * s + h][0:NP, t * (C + 1):(t + 1) * (C + 1)], st[s][:, h, t, :], vmat[:, h, :],
                                                    start=True, stop=True)
                    last.then_inc(pr_ready, 1)

                def turn(b, s):
                    wait_apart(pe, norm_ready, b + 1)
                    if not (isinstance(b, int) and b == 0):
                        wait_apart(pe, oT_sb, b)
                    for t in range(OT):
                        last = nc.tensor.transpose(banks[4][0:C, t * NP:(t + 1) * NP], on[s][:, t, :], ident[0:NP, 0:NP])
                    last.then_inc(oT_ps, 1)

                def second(b, s):
                    pe.wait_ge(hid_sb, b + 1)
                    if not (isinstance(b, int) and b < 2):
                        pe.wait_ge(fin_ready, b - 1)
                    for t in range(OT):
                        last = nc.tensor.matmul(banks[6 + s][0:NP, t * C:(t + 1) * C], hT[s][:, t * NP:(t + 1) * NP], w2[:, :],
                                                start=True, stop=True)
                    last.then_inc(y_ps, 1)

                def first(b, s):
                    wait_apart(pe, oT_sb, b + 1)
                    if not (isinstance(b, int) and b == 0):
                        wait_apart(pe, hid_sb, b)
                    nc.tensor.matmul(banks[5][0:C, 0:OT * NP], w1[:, :], oT[s], start=True, stop=True).then_inc(hid_ps, 1)

                def slot(g, s, b, z, half, e):
                    if there(g):
                        project(g, s)
                    if there(b):
                        turn(b, z)
                    if there(b - 1):
                        second(b - 1, 1 - z)
                    if there(b):
                        first(b, z)

                slots(pe, slot)

            @block.vector
            def _(dve):
                def centre(g, s):
                    n = [0]

                    def link(ins):
                        n[0] += 1
                        ins.then_inc(dve_c, 1)
                        dve.wait_ge(dve_c, g * LINKS + n[0])
                    dve.wait_ge(pr_ready, g + 1)
                    pr = [banks[2 * s + h][0:NP, 0:OT * (C + 1)].rearrange("p (t c) -> p t c", c=C + 1) for h in range(H)]
                    for h in range(H):
                        link(nc.vector.tensor_scalar(den[s][:, h, :], pr[h][:, :, C], 1e-8, None, ALU.add))
                    link(nc.vector.reciprocal(den_r[s], den[s]))
                    if not (isinstance(g, int) and g < 2):
                        dve.wait_ge(ox_ready, g - 1)
                    for h, to in enumerate((oo[s], o1[s])):
                        nc.vector.tensor_tensor(to, pr[h][:, :, 0:C], den_r[s][:, h, :].unsqueeze(2).broadcast_to([NP, OT, C]),
                                                ALU.mult).then_inc(pr_read, 1)
                    dve.wait_ge(pr_read, g * H + H)
                    link(nc.vector.tensor_tensor(oo[s], oo[s], o1[s], ALU.add))
                    dve.wait_ge(hbp_ready, g + 1)
                    nc.vector.tensor_tensor(oo[s], oo[s], hb[s], ALU.add).then_inc(o_ready, 1)
                    dve.wait_ge(o_ready, g + 1)
                    link(nc.vector.tensor_reduce(mean[s], oo[s], X_AXIS, ALU.add))
                    link(nc.vector.tensor_scalar(mean[s], mean[s], 1.0 / C, None, ALU.mult))
                    nc.vector.tensor_tensor(of(oc, g), oo[s], mean[s].unsqueeze(2).broadcast_to([NP, OT, C]), ALU.subtract)\
                      .then_inc(oc_ready, 1)
                    assert n[0] == LINKS, n[0]

                def variance(g, s):
                    dve.wait_ge(sq_ready, g + 1)
                    nc.vector.tensor_reduce(of(var, g), osq[s], X_AXIS, ALU.add).then_inc(var_ready, 1)

                def end_round(e, g):
                    n = 1 if isinstance(e, int) and e == 0 else 2
                    dve.wait_ge(sd_ready, e + 1)
                    nc.vector.memset(spare[:, :], 0.0)
                    v = of(var, g - (n - 1), n)
                    nc.vector.reciprocal(v, v).then_inc(inv_ready, 1)
                    dve.wait_ge(inv_ready, e + 1)

                def normalise(b, s):
                    if not (isinstance(b, int) and b < 2):
                        dve.wait_ge(oT_ps, b - 1)
                    nc.vector.tensor_tensor(on[s], of(oc, b), of(var, b).unsqueeze(2).broadcast_to([NP, OT, C]), ALU.mult)\
                      .then_inc(norm_ready, 1)

                def finish(b, s, half):
                    dve.wait_ge(y_ps, b + 1)
                    dve.wait_ge(ox_ready, b + 1)
                    if not isinstance(b, int) or b > 1:
                        dve.wait_ge(out_done[s], half * 32)
                    nc.vector.tensor_tensor(fin[s], banks[6 + s][0:NP, 0:OT * C].rearrange("p (t c) -> p t c", c=C), of(ob, b),
                                            ALU.add).then_inc(fin_ready, 1)

                def slot(g, s, b, z, half, e):
                    if there(g):
                        centre(g, s)
                    if there(b - 1):
                        finish(b - 1, 1 - z, half)
                    if there(g):
                        variance(g, s)
                    if e is not None:
                        end_round(e, g)
                    if there(b + 1):
                        normalise(b + 1, 1 - z)

                slots(dve, slot)

    return nc


_INS = ["x", "src", "dst", "edge_attr_32"] + [
    "L0_gnn_" + n for n in ("Wq", "bq", "Wk", "bk", "Wv", "bv", "We", "Wp", "bp", "ln1_g", "ln1_b", "ln2_g", "ln2_b",
                            "W1", "b1", "W2", "b2")]


def kernel(**inputs):
    import concourse.bacc as _bacc
    from concourse.bass_utils import run_bass_kernel_spmd as _run

    nc = _bacc.Bacc("TRN2", target_bir_lowering=False, num_devices=1)
    arrays, args = {}, []
    for name in _INS:
        a = np.ascontiguousarray(inputs[name])
        arrays[f"in_{name}"] = a
        args.append(nc.dram_tensor(f"in_{name}", a.shape, mybir.dt.from_np(a.dtype), kind="ExternalInput").ap())
    out = nc.dram_tensor("out_0", (N, C), F32, kind="ExternalOutput").ap()
    gnn_kernel(nc, *args, out)
    return _run(nc, [arrays], core_ids=[0]).results[0]["out_0"]
```
